# Optimizing a Trainium2 kernel written in Bass

```python
import numpy as np
import jax
import jax.numpy as jnp

def _softmax(x, axis=-1):
    return jax.nn.softmax(x, axis=axis)

def _gelu(x):
    return jax.nn.gelu(x, approximate=True)

def _silu(x):
    return jax.nn.silu(x)

def _sigmoid(x):
    return jax.nn.sigmoid(x)

def _layernorm(x, axis=-1, eps=1e-05):
    m = jnp.mean(x, axis=axis, keepdims=True)
    v = jnp.var(x, axis=axis, keepdims=True)
    return (x - m) / jnp.sqrt(v + eps)

def _scatter_add(tgt, idx, src, axis=0):
    return tgt.at[idx].add(src)

def _segment_sum(src, seg, n):
    return jax.ops.segment_sum(src, seg, n)
kernel_name = 'mk_flamingo_gated_d2_seqx_r4_9e1959'

def setup_inputs(seed: int=0):
    np.random.seed(seed)
    _w = jnp.asarray

    def _rec_inputs():
        import jax
        import jax.numpy as jnp
        _rk = jax.random.key(seed)
        x = -0.0002928 + 1 * jax.random.normal(jax.random.fold_in(_rk, 1), (2, 512, 256), jnp.float32)
        _lenS = 512 - jax.random.randint(jax.random.fold_in(_rk, 7), (2,), 0, max(1, 512 // 4) + 1, jnp.int32)
        _lenS2 = 1024 - jax.random.randint(jax.random.fold_in(_rk, 8), (2,), 0, max(1, 1024 // 4) + 1, jnp.int32)
        _ctx_1024P = jax.random.normal(jax.random.fold_in(_rk, 11), (2, 16, 256), jnp.float32)
        _ctx_1024c = jax.random.dirichlet(jax.random.fold_in(_rk, 511), 0.3 * jnp.ones((16,), jnp.float32), (2, 1024))
        _ctx_1024t = jnp.einsum('bsk,bkd->bsd', _ctx_1024c, _ctx_1024P)
        _ctx_1024t = _ctx_1024t * jax.lax.rsqrt(jnp.mean(jnp.square(_ctx_1024t)) + 1e-12) * 0.953939
        ctx_1024 = 4.13588e-05 + 0.999923 * (_ctx_1024t + 0.3 * jax.random.normal(jax.random.fold_in(_rk, 611), (2, 1024, 256), jnp.float32))
        _validS = jnp.arange(512)[None, :] < _lenS[:, None]
        _validS2 = jnp.arange(1024)[None, :] < _lenS2[:, None]
        _causal = jnp.tril(jnp.ones((512, 512), dtype=bool))
        mask_Bx1x1xS2_ff0 = jnp.where(jnp.ones((2, 1, 1, 1024), dtype=bool), 0.0, -1000000000.0).astype(jnp.float32)
        _g = jax.random.normal(jax.random.fold_in(_rk, 9001), (2, 2), jnp.float32)
        _g = jnp.sign(_g) * jnp.maximum(jnp.abs(_g), 1.0) + (_g == 0) * 1.0
        g_xattn = _g[0]
        g_ffn = _g[1]
        return (x, ctx_1024, mask_Bx1x1xS2_ff0, g_xattn, g_ffn)
    x, ctx_1024, mask_Bx1x1xS2_ff0, g_xattn, g_ffn = _rec_inputs()

    def _L0_xattn_setup():
        import jax, jax.numpy as jnp
        import numpy as np
        H = 16
        D = 256
        F = 1024
        LN_EPS = 1e-05

        def _glorot(key, shape):
            fan_in, fan_out = (shape[0], shape[1])
            lim = np.sqrt(6.0 / (fan_in + fan_out))
            return jax.random.uniform(key, shape, jnp.float32, -lim, lim)

        def _split_heads(x):
            b, l, _ = x.shape
            return x.reshape(b, l, H, D // H)

        def _mha(x, ctx, mask, qw, qb, kw, kb, vw, vb):
            q = _split_heads(x @ qw + qb)
            k = _split_heads(ctx @ kw + kb)
            v = _split_heads(ctx @ vw + vb)
            scores = jnp.einsum('bqhd,bkhd->bhqk', q, k) / np.sqrt(D // H).astype(np.float32)
            if mask is not None:
                scores = scores + mask
            probs = jax.nn.softmax(scores, axis=-1)
            out = jnp.einsum('bhqk,bkhd->bqhd', probs, v)
            return out.reshape(x.shape[0], x.shape[1], D)

        def _self_output(h, residual, w, b, g, be):
            h = h @ w + b
            h = h + residual
            mu = jnp.mean(h, axis=-1, keepdims=True)
            var = jnp.mean(jnp.square(h - mu), axis=-1, keepdims=True)
            return (h - mu) * jax.lax.rsqrt(var + LN_EPS) * g + be
        key = jax.random.key(seed)
        ks = jax.random.split(key, 16)
        inp = {'input_tensor': jax.random.normal(ks[0], (4, 256, D), jnp.float32), 'ctx_tensor': jax.random.normal(ks[1], (4, 512, D), jnp.float32), 'ctx_attn_mask': jnp.zeros((4, 1, 1, 512), jnp.float32), 'cq_w': _glorot(ks[2], (D, D)), 'cq_b': jnp.zeros((D,)), 'ck_w': _glorot(ks[3], (D, D)), 'ck_b': jnp.zeros((D,)), 'cv_w': _glorot(ks[4], (D, D)), 'cv_b': jnp.zeros((D,)), 'co_w': _glorot(ks[5], (D, D)), 'co_b': jnp.zeros((D,)), 'co_g': jnp.ones((D,)), 'co_be': jnp.zeros((D,)), 'sq_w': _glorot(ks[6], (D, D)), 'sq_b': jnp.zeros((D,)), 'sk_w': _glorot(ks[7], (D, D)), 'sk_b': jnp.zeros((D,)), 'sv_w': _glorot(ks[8], (D, D)), 'sv_b': jnp.zeros((D,)), 'so_w': _glorot(ks[9], (D, D)), 'so_b': jnp.zeros((D,)), 'so_g': jnp.ones((D,)), 'so_be': jnp.zeros((D,)), 'fi_w': _glorot(ks[10], (D, F)), 'fi_b': jnp.zeros((F,)), 'fo_w': _glorot(ks[11], (F, D)), 'fo_b': jnp.zeros((D,)), 'fo_g': jnp.ones((D,)), 'fo_be': jnp.zeros((D,))}
        return inp
    _L0_xattn_all = _L0_xattn_setup()
    _L0_xattn_in = {k: v for k, v in _L0_xattn_all.items() if k in ('cq_w', 'cq_b', 'ck_w', 'ck_b', 'cv_w', 'cv_b', 'co_w', 'co_b', 'co_g', 'co_be', 'sq_w', 'sq_b', 'sk_w', 'sk_b', 'sv_w', 'sv_b', 'so_w', 'so_b', 'so_g', 'so_be', 'fi_w', 'fi_b', 'fo_w', 'fo_b', 'fo_g', 'fo_be')}
    del _L0_xattn_all

    def _L0_ffn_setup():
        import jax, jax.numpy as jnp
        import numpy as np
        BLOCK = 16
        _GRID = jnp.array([0.0, 0.5, 1.0, 1.5, 2.0, 3.0, 4.0, 6.0], dtype=jnp.float32)
        _MID = jnp.array([0.25, 0.75, 1.25, 1.75, 2.5, 3.5, 5.0], dtype=jnp.float32)

        def fp4_quant_dequant(x):
            shape = x.shape
            xb = x.reshape(shape[:-1] + (shape[-1] // BLOCK, BLOCK))
            scale = jnp.max(jnp.abs(xb), axis=-1, keepdims=True) / 6.0
            scale = jnp.maximum(scale, jnp.float32(1e-12))
            xn = xb / scale
            idx = jnp.searchsorted(_MID, jnp.abs(xn))
            q = _GRID[idx] * jnp.sign(xn) * scale
            return q.reshape(shape)

        def fp4_linear(x, w):
            xq = fp4_quant_dequant(x)
            wq = fp4_quant_dequant(w)
            return jnp.einsum('bsk,nk->bsn', xq, wq)
        key = jax.random.key(seed)
        k1, k2, k3, k4 = jax.random.split(key, 4)
        H, I = (256, 704)
        x = jax.random.normal(k1, (4, 1024, H), dtype=jnp.float32)
        w_gate = jax.random.normal(k2, (I, H), dtype=jnp.float32) * 0.02
        w_up = jax.random.normal(k3, (I, H), dtype=jnp.float32) * 0.02
        w_down = jax.random.normal(k4, (H, I), dtype=jnp.float32) * 0.02
        return {'x': x, 'w_gate': w_gate, 'w_up': w_up, 'w_down': w_down}
    _L0_ffn_all = _L0_ffn_setup()
    _L0_ffn_in = {k: v for k, v in _L0_ffn_all.items() if k in ('w_gate', 'w_up', 'w_down')}
    del _L0_ffn_all

    def _L1_xattn_setup():
        import jax, jax.numpy as jnp
        import numpy as np
        HEADS = 8
        DIM_HEAD = 64
        DIM = 256
        CTX_DIM = 256
        HIDDEN = HEADS * DIM_HEAD
        key = jax.random.key(seed)
        ks = jax.random.split(key, 7)
        b, n, m = (2, 512, 512)
        x = jax.random.normal(ks[0], (b, n, DIM), dtype=jnp.float32)
        context = jax.random.normal(ks[1], (b, m, CTX_DIM), dtype=jnp.float32)
        Wq = jax.random.normal(ks[2], (DIM, HIDDEN), dtype=jnp.float32) * (1.0 / np.sqrt(DIM))
        Wk = jax.random.normal(ks[3], (CTX_DIM, HIDDEN), dtype=jnp.float32) * (1.0 / np.sqrt(CTX_DIM))
        Wv = jax.random.normal(ks[4], (CTX_DIM, HIDDEN), dtype=jnp.float32) * (1.0 / np.sqrt(CTX_DIM))
        Wo = jax.random.normal(ks[5], (HIDDEN, DIM), dtype=jnp.float32) * (1.0 / np.sqrt(HIDDEN))
        bo = jax.random.normal(ks[6], (DIM,), dtype=jnp.float32) * 0.01
        return {'x': x, 'context': context, 'Wq': Wq, 'Wk': Wk, 'Wv': Wv, 'Wo': Wo, 'bo': bo}
    _L1_xattn_all = _L1_xattn_setup()
    _L1_xattn_in = {k: v for k, v in _L1_xattn_all.items() if k in ('Wq', 'Wk', 'Wv', 'Wo', 'bo')}
    del _L1_xattn_all

    def _L1_ffn_setup():
        import jax, jax.numpy as jnp
        import numpy as np
        E, K = (8, 4)
        B, S, D = (4, 256, 256)
        H = D * 2 * 4 // 3

        def _swiglu(u, w1, w2, w3):
            h = jnp.einsum('...d,hd->...h', u, w1)
            v = jnp.einsum('...d,hd->...h', u, w2)
            return jnp.einsum('...h,dh->...d', jax.nn.sigmoid(h) * h * v, w3)
        key = jax.random.key(seed)
        ks = jax.random.split(key, 9)
        std = 0.02
        return {'x': jax.random.normal(ks[0], (B, S, D), jnp.float32), 'Wg': jax.random.normal(ks[1], (E, D), jnp.float32) * std, 'routing_bias': jnp.zeros((E,), jnp.float32), 'W1': jax.random.normal(ks[2], (E, H, D), jnp.float32) * std, 'W2': jax.random.normal(ks[3], (E, H, D), jnp.float32) * std, 'W3': jax.random.normal(ks[4], (E, D, H), jnp.float32) * std, 'Ws1': jax.random.normal(ks[5], (H, D), jnp.float32) * std, 'Ws2': jax.random.normal(ks[6], (H, D), jnp.float32) * std, 'Ws3': jax.random.normal(ks[7], (D, H), jnp.float32) * std}
    _L1_ffn_all = _L1_ffn_setup()
    _L1_ffn_in = {k: v for k, v in _L1_ffn_all.items() if k in ('Wg', 'routing_bias', 'W1', 'W2', 'W3', 'Ws1', 'Ws2', 'Ws3')}
    del _L1_ffn_all
    return {'x': x, 'ctx_1024': ctx_1024, 'mask_Bx1x1xS2_ff0': mask_Bx1x1xS2_ff0, 'g_xattn': g_xattn, 'g_ffn': g_ffn, 'L0_xattn_cq_w': _L0_xattn_in['cq_w'], 'L0_xattn_cq_b': _L0_xattn_in['cq_b'], 'L0_xattn_ck_w': _L0_xattn_in['ck_w'], 'L0_xattn_ck_b': _L0_xattn_in['ck_b'], 'L0_xattn_cv_w': _L0_xattn_in['cv_w'], 'L0_xattn_cv_b': _L0_xattn_in['cv_b'], 'L0_xattn_co_w': _L0_xattn_in['co_w'], 'L0_xattn_co_b': _L0_xattn_in['co_b'], 'L0_xattn_co_g': _L0_xattn_in['co_g'], 'L0_xattn_co_be': _L0_xattn_in['co_be'], 'L0_xattn_sq_w': _L0_xattn_in['sq_w'], 'L0_xattn_sq_b': _L0_xattn_in['sq_b'], 'L0_xattn_sk_w': _L0_xattn_in['sk_w'], 'L0_xattn_sk_b': _L0_xattn_in['sk_b'], 'L0_xattn_sv_w': _L0_xattn_in['sv_w'], 'L0_xattn_sv_b': _L0_xattn_in['sv_b'], 'L0_xattn_so_w': _L0_xattn_in['so_w'], 'L0_xattn_so_b': _L0_xattn_in['so_b'], 'L0_xattn_so_g': _L0_xattn_in['so_g'], 'L0_xattn_so_be': _L0_xattn_in['so_be'], 'L0_xattn_fi_w': _L0_xattn_in['fi_w'], 'L0_xattn_fi_b': _L0_xattn_in['fi_b'], 'L0_xattn_fo_w': _L0_xattn_in['fo_w'], 'L0_xattn_fo_b': _L0_xattn_in['fo_b'], 'L0_xattn_fo_g': _L0_xattn_in['fo_g'], 'L0_xattn_fo_be': _L0_xattn_in['fo_be'], 'L0_ffn_w_gate': _L0_ffn_in['w_gate'], 'L0_ffn_w_up': _L0_ffn_in['w_up'], 'L0_ffn_w_down': _L0_ffn_in['w_down'], 'L1_xattn_Wq': _L1_xattn_in['Wq'], 'L1_xattn_Wk': _L1_xattn_in['Wk'], 'L1_xattn_Wv': _L1_xattn_in['Wv'], 'L1_xattn_Wo': _L1_xattn_in['Wo'], 'L1_xattn_bo': _L1_xattn_in['bo'], 'L1_ffn_Wg': _L1_ffn_in['Wg'], 'L1_ffn_routing_bias': _L1_ffn_in['routing_bias'], 'L1_ffn_W1': _L1_ffn_in['W1'], 'L1_ffn_W2': _L1_ffn_in['W2'], 'L1_ffn_W3': _L1_ffn_in['W3'], 'L1_ffn_Ws1': _L1_ffn_in['Ws1'], 'L1_ffn_Ws2': _L1_ffn_in['Ws2'], 'L1_ffn_Ws3': _L1_ffn_in['Ws3']}

def reference(x, ctx_1024, mask_Bx1x1xS2_ff0, g_xattn, g_ffn, L0_xattn_cq_w, L0_xattn_cq_b, L0_xattn_ck_w, L0_xattn_ck_b, L0_xattn_cv_w, L0_xattn_cv_b, L0_xattn_co_w, L0_xattn_co_b, L0_xattn_co_g, L0_xattn_co_be, L0_xattn_sq_w, L0_xattn_sq_b, L0_xattn_sk_w, L0_xattn_sk_b, L0_xattn_sv_w, L0_xattn_sv_b, L0_xattn_so_w, L0_xattn_so_b, L0_xattn_so_g, L0_xattn_so_be, L0_xattn_fi_w, L0_xattn_fi_b, L0_xattn_fo_w, L0_xattn_fo_b, L0_xattn_fo_g, L0_xattn_fo_be, L0_ffn_w_gate, L0_ffn_w_up, L0_ffn_w_down, L1_xattn_Wq, L1_xattn_Wk, L1_xattn_Wv, L1_xattn_Wo, L1_xattn_bo, L1_ffn_Wg, L1_ffn_routing_bias, L1_ffn_W1, L1_ffn_W2, L1_ffn_W3, L1_ffn_Ws1, L1_ffn_Ws2, L1_ffn_Ws3):
    import jax
    import jax.numpy as jnp

    def _L0_xattn_ref(input_tensor, ctx_tensor, ctx_attn_mask, cq_w, cq_b, ck_w, ck_b, cv_w, cv_b, co_w, co_b, co_g, co_be, sq_w, sq_b, sk_w, sk_b, sv_w, sv_b, so_w, so_b, so_g, so_be, fi_w, fi_b, fo_w, fo_b, fo_g, fo_be):
        import jax, jax.numpy as jnp
        import numpy as np
        H = 16
        D = 256
        F = 1024
        LN_EPS = 1e-05

        def _glorot(key, shape):
            fan_in, fan_out = (shape[0], shape[1])
            lim = np.sqrt(6.0 / (fan_in + fan_out))
            return jax.random.uniform(key, shape, jnp.float32, -lim, lim)

        def _split_heads(x):
            b, l, _ = x.shape
            return x.reshape(b, l, H, D // H)

        def _mha(x, ctx, mask, qw, qb, kw, kb, vw, vb):
            q = _split_heads(x @ qw + qb)
            k = _split_heads(ctx @ kw + kb)
            v = _split_heads(ctx @ vw + vb)
            scores = jnp.einsum('bqhd,bkhd->bhqk', q, k) / np.sqrt(D // H).astype(np.float32)
            if mask is not None:
                scores = scores + mask
            probs = jax.nn.softmax(scores, axis=-1)
            out = jnp.einsum('bhqk,bkhd->bqhd', probs, v)
            return out.reshape(x.shape[0], x.shape[1], D)

        def _self_output(h, residual, w, b, g, be):
            h = h @ w + b
            h = h + residual
            mu = jnp.mean(h, axis=-1, keepdims=True)
            var = jnp.mean(jnp.square(h - mu), axis=-1, keepdims=True)
            return (h - mu) * jax.lax.rsqrt(var + LN_EPS) * g + be
        ca = _mha(input_tensor, ctx_tensor, ctx_attn_mask, cq_w, cq_b, ck_w, ck_b, cv_w, cv_b)
        x = _self_output(ca, input_tensor, co_w, co_b, co_g, co_be)
        sa = _mha(x, x, None, sq_w, sq_b, sk_w, sk_b, sv_w, sv_b)
        x = _self_output(sa, x, so_w, so_b, so_g, so_be)
        inter = jax.nn.gelu(x @ fi_w + fi_b, approximate=False)
        x = _self_output(inter, x, fo_w, fo_b, fo_g, fo_be)
        return x

    def _L0_ffn_ref(x, w_gate, w_up, w_down):
        import jax, jax.numpy as jnp
        import numpy as np
        BLOCK = 16
        _GRID = jnp.array([0.0, 0.5, 1.0, 1.5, 2.0, 3.0, 4.0, 6.0], dtype=jnp.float32)
        _MID = jnp.array([0.25, 0.75, 1.25, 1.75, 2.5, 3.5, 5.0], dtype=jnp.float32)

        def fp4_quant_dequant(x):
            shape = x.shape
            xb = x.reshape(shape[:-1] + (shape[-1] // BLOCK, BLOCK))
            scale = jnp.max(jnp.abs(xb), axis=-1, keepdims=True) / 6.0
            scale = jnp.maximum(scale, jnp.float32(1e-12))
            xn = xb / scale
            idx = jnp.searchsorted(_MID, jnp.abs(xn))
            q = _GRID[idx] * jnp.sign(xn) * scale
            return q.reshape(shape)

        def fp4_linear(x, w):
            xq = fp4_quant_dequant(x)
            wq = fp4_quant_dequant(w)
            return jnp.einsum('bsk,nk->bsn', xq, wq)
        gate = fp4_linear(x, w_gate)
        y = fp4_linear(x, w_up)
        h = jax.nn.silu(gate) * y
        return fp4_linear(h, w_down)

    def _L1_xattn_ref(x, context, Wq, Wk, Wv, Wo, bo):
        import jax, jax.numpy as jnp
        import numpy as np
        HEADS = 8
        DIM_HEAD = 64
        DIM = 256
        CTX_DIM = 256
        HIDDEN = HEADS * DIM_HEAD
        b, n, _ = x.shape
        m = context.shape[1]
        scale = DIM_HEAD ** (-0.5)
        q = (x @ Wq).reshape(b, n, HEADS, DIM_HEAD).transpose(0, 2, 1, 3)
        k = (context @ Wk).reshape(b, m, HEADS, DIM_HEAD).transpose(0, 2, 1, 3)
        v = (context @ Wv).reshape(b, m, HEADS, DIM_HEAD).transpose(0, 2, 1, 3)
        scores = jnp.einsum('bhnd,bhmd->bhnm', q, k) * scale
        attn = jax.nn.softmax(scores, axis=-1)
        out = jnp.einsum('bhnm,bhmd->bhnd', attn, v)
        out = out.transpose(0, 2, 1, 3).reshape(b, n, HIDDEN)
        return out @ Wo + bo

    def _L1_ffn_ref(x, Wg, routing_bias, W1, W2, W3, Ws1, Ws2, Ws3):
        import jax, jax.numpy as jnp
        import numpy as np
        E, K = (8, 4)
        B, S, D = (4, 256, 256)
        H = D * 2 * 4 // 3

        def _swiglu(u, w1, w2, w3):
            h = jnp.einsum('...d,hd->...h', u, w1)
            v = jnp.einsum('...d,hd->...h', u, w2)
            return jnp.einsum('...h,dh->...d', jax.nn.sigmoid(h) * h * v, w3)
        gate = jnp.einsum('bsd,ed->bse', x, Wg) + routing_bias
        _, top_idx = jax.lax.top_k(gate, K)
        mask = jax.nn.one_hot(top_idx, E, dtype=gate.dtype).sum(-2)
        masked_gate = jnp.where(mask > 0, gate, -jnp.inf)
        probs = jax.nn.softmax(masked_gate, axis=-1)
        weights = probs * mask
        out = _swiglu(x, Ws1, Ws2, Ws3)
        h1 = jnp.einsum('bsd,ehd->ebsh', x, W1)
        h2 = jnp.einsum('bsd,ehd->ebsh', x, W2)
        eo = jnp.einsum('ebsh,edh->ebsd', jax.nn.sigmoid(h1) * h1 * h2, W3)
        out = out + jnp.einsum('ebsd,bse->bsd', eo, weights)
        return out
    x = x + jnp.tanh(g_xattn[0]) * _L0_xattn_ref(_layernorm(x, axis=-1), ctx_1024, mask_Bx1x1xS2_ff0, L0_xattn_cq_w, L0_xattn_cq_b, L0_xattn_ck_w, L0_xattn_ck_b, L0_xattn_cv_w, L0_xattn_cv_b, L0_xattn_co_w, L0_xattn_co_b, L0_xattn_co_g, L0_xattn_co_be, L0_xattn_sq_w, L0_xattn_sq_b, L0_xattn_sk_w, L0_xattn_sk_b, L0_xattn_sv_w, L0_xattn_sv_b, L0_xattn_so_w, L0_xattn_so_b, L0_xattn_so_g, L0_xattn_so_be, L0_xattn_fi_w, L0_xattn_fi_b, L0_xattn_fo_w, L0_xattn_fo_b, L0_xattn_fo_g, L0_xattn_fo_be)
    x = x + jnp.tanh(g_ffn[0]) * _L0_ffn_ref(_layernorm(x, axis=-1), L0_ffn_w_gate, L0_ffn_w_up, L0_ffn_w_down)
    x = x + jnp.tanh(g_xattn[1]) * _L1_xattn_ref(_layernorm(x, axis=-1), ctx_1024, L1_xattn_Wq, L1_xattn_Wk, L1_xattn_Wv, L1_xattn_Wo, L1_xattn_bo)
    x = x + jnp.tanh(g_ffn[1]) * _L1_ffn_ref(_layernorm(x, axis=-1), L1_ffn_Wg, L1_ffn_routing_bias, L1_ffn_W1, L1_ffn_W2, L1_ffn_W3, L1_ffn_Ws1, L1_ffn_Ws2, L1_ffn_Ws3)
    return x

_drawn_inputs = setup_inputs


def setup_inputs(seed=0):
    import zlib

    import numpy as np

    out = dict(_drawn_inputs(seed))
    spreads = {'g_ffn': (-1.0, 0.6),
     'L0_xattn_cq_b': (0.0, 0.8),
     'L0_xattn_ck_b': (0.0, 0.8),
     'L0_xattn_cv_b': (0.0, 0.1),
     'L0_xattn_co_b': (0.0, 0.1),
     'L0_xattn_co_g': (1.0, 0.2),
     'L0_xattn_co_be': (0.0, 0.1),
     'L0_xattn_sq_b': (0.0, 0.8),
     'L0_xattn_sk_b': (0.0, 0.8),
     'L0_xattn_sv_b': (0.0, 0.1),
     'L0_xattn_so_b': (0.0, 0.1),
     'L0_xattn_so_g': (1.0, 0.2),
     'L0_xattn_so_be': (0.0, 0.1),
     'L0_xattn_fi_b': (0.0, 0.1),
     'L0_xattn_fo_b': (0.0, 0.1),
     'L0_xattn_fo_g': (1.0, 0.2),
     'L0_xattn_fo_be': (0.0, 0.1),
     'L1_ffn_routing_bias': (0.0, 0.8)}
    factors = {'L0_ffn_w_gate': 3.884,
     'L0_ffn_w_up': 3.453,
     'L0_ffn_w_down': 3.424,
     'L1_xattn_bo': 8.0,
     'L1_ffn_Wg': 8.0,
     'L1_ffn_W1': 8.0,
     'L1_ffn_W2': 8.0,
     'L1_ffn_W3': 8.0,
     'L1_ffn_Ws1': 4.214,
     'L1_ffn_Ws2': 4.123,
     'L1_ffn_Ws3': 4.121}
    for name, (base, spread) in spreads.items():
        noise = np.random.default_rng([zlib.crc32(name.encode()), seed]).standard_normal(out[name].shape)
        drawn = base * np.exp(spread * noise) if base else spread * noise
        out[name] = jnp.asarray(drawn.astype(out[name].dtype))
    for name, factor in factors.items():
        out[name] = (out[name] * factor).astype(out[name].dtype)
    return out
```

```python
from contextlib import ExitStack, contextmanager

import concourse.bass as bass
from concourse import mybir

F32 = mybir.dt.float32
F16 = mybir.dt.float16
BF16 = mybir.dt.bfloat16
U32 = mybir.dt.uint32
ALU = mybir.AluOpType
ACT = mybir.ActivationFunctionType
AX = mybir.AxisListType

P = 128
B, NQ, NCTX, D = 2, 512, 1024, 256
T = B * NQ
TT = T // P
QT = NQ // P
KC = D // P
BANK = 512
EPS = 1e-5
LN_P_SCALE = 10 * 0.6931471805599453

FP4_BLOCK = 16
SPLIT_TWO_BITS = 4194305.0
HALF_GRID = 6291456.0
TIE_DOWN = 1.0 - 2.0 ** -23


class Signal:

    def __init__(self, sem):
        self.sem = sem
        self.base = 0

    def at(self, n):
        return self.base + n

    def close(self, n):
        self.base += n


class Chain:

    def __init__(self, sem):
        self.sem = sem
        self.count = 0
        self.offset = None

    def step(self, eng, ins):
        ins.then_inc(self.sem, 1)
        self.count += 1
        eng.wait_ge(self.sem, self.count if self.offset is None else self.offset + self.count)

    @contextmanager
    def loop(self, i, steps, trips):
        before = self.count
        self.offset = i * steps
        yield
        assert self.count == before + steps, (self.count - before, steps)
        self.offset = None
        self.count = before + steps * trips


class Machine:

    def __init__(self, nc, ctx):
        self.nc = nc
        self.ctx = ctx

        def signal(name):
            return Signal(ctx.enter_context(nc.semaphore(name)))

        self.loaded = signal("loaded")
        self.stored = signal("stored")
        self.products = signal("products")
        self.high_done = signal("high_done")
        self.low_done = signal("low_done")
        self.evacuated = signal("evacuated")
        self.variance = signal("variance")
        self.deviation = signal("deviation")
        self.ready = signal("ready")
        self.act_ready = signal("act_ready")
        self.operands = (signal("operands_even"), signal("operands_odd"))
        self.maxima = signal("maxima")
        self.probs = signal("probs")
        self.scores = signal("scores")
        self.probs_t = signal("probs_t")
        self.weighted = signal("weighted")
        self.finished = signal("finished")
        self.down_done = signal("down_done")
        self.w12_loaded = signal("w12_loaded")
        self.w3_loaded = signal("w3_loaded")
        self.w12_high = signal("w12_high")
        self.w12_low = signal("w12_low")
        self.w3_high = signal("w3_high")
        self.w3_low = signal("w3_low")
        self.vchain = Chain(ctx.enter_context(nc.semaphore("vchain")))
        self.achain = Chain(ctx.enter_context(nc.semaphore("achain")))
        self.pchain = Chain(ctx.enter_context(nc.semaphore("pchain")))
        ahead = (self.evacuated, self.down_done, self.w12_low, self.w3_low, self.products,
                 self.weighted, self.low_done, self.high_done, self.scores, self.probs, self.finished)
        with nc.Block(no_gpsimd_drain=True) as block:
            @block.sync
            def _(sp):
                for s in ahead:
                    sp.sem_inc(s.sem, 1)
        for s in ahead:
            s.close(1)
        self.psum = ctx.enter_context(nc.psum_tensor("psum", [P, 8, BANK], F32))

    def block(self):
        return self.nc.Block(no_gpsimd_drain=True)


def three_terms(pe, out, w_hi, w_lo, x_hi, x_lo, first, last):
    pe.matmul(out, w_hi, x_hi, start=first, stop=False)
    pe.matmul(out, w_hi, x_lo, start=False, stop=False)
    return pe.matmul(out, w_lo, x_hi, start=False, stop=last)


def load_split(m, items):
    with m.block() as block:
        @block.sync
        def _(sp):
            for staging, source, _, _ in items:
                sp.dma_start(staging, source).then_inc(m.loaded.sem, 16)

        @block.scalar
        def _(act):
            act.wait_ge(m.loaded.sem, m.loaded.at(16 * len(items)))
            for staging, _, high, _ in items:
                act.activation(high, staging, ACT.Copy).then_inc(m.high_done.sem, 1)

        @block.vector
        def _(dve):
            for n, (staging, _, high, low) in enumerate(items):
                dve.wait_ge(m.high_done.sem, m.high_done.at(n + 1))
                dve.tensor_tensor(low, staging, high, ALU.subtract)

    m.loaded.close(16 * len(items))
    m.high_done.close(len(items))


def layer_norm(m, tmp, src, dst, gamma=None, beta=None):
    stats, mv, rstd = tmp["stats"], tmp["mv"], tmp["rstd"]
    with m.block() as block:
        @block.vector
        def _(dve):
            for t in range(TT):
                dve.bn_stats(stats[:, t, :], src[:, t, :]).then_inc(m.ready.sem, 1)
            for t in range(TT):
                dve.wait_ge(m.ready.sem, m.ready.at(t + 1))
                dve.bn_aggr(mv[:, t, :], stats[:, t, :]).then_inc(m.ready.sem, 1)
            dve.wait_ge(m.ready.sem, m.ready.at(2 * TT))
            dve.tensor_scalar(rstd[:, :], mv[:, :, 1], EPS, None, ALU.add).then_inc(m.variance.sem, 1)
            dve.wait_ge(m.deviation.sem, m.deviation.at(1))
            m.vchain.step(dve, dve.reciprocal(rstd[:, :], rstd[:, :]))
            for t in range(TT):
                out = dve.tensor_scalar(dst[:, t, :], src[:, t, :], mv[:, t, 0:1], rstd[:, t:t + 1],
                                        ALU.subtract, ALU.mult)
                if gamma is not None:
                    m.vchain.step(dve, out)
                    m.vchain.step(dve, dve.tensor_tensor(dst[:, t, :], dst[:, t, :], gamma, ALU.mult))
                    dve.tensor_tensor(dst[:, t, :], dst[:, t, :], beta, ALU.add)

        @block.scalar
        def _(act):
            act.wait_ge(m.variance.sem, m.variance.at(1))
            act.activation(rstd[:, :], rstd[:, :], ACT.Sqrt).then_inc(m.deviation.sem, 1)

    m.ready.close(2 * TT)
    m.variance.close(1)
    m.deviation.close(1)


def transpose_split(m, ident, source, chunks, high, low):
    banks = (len(chunks) + 3) // 4
    slots = 8 // banks
    with m.block() as block:
        @block.tensor
        def _(pe):
            for t in range(TT):
                if t >= slots:
                    pe.wait_ge(m.low_done.sem, m.low_done.at(t - slots + 1))
                for c, width in enumerate(chunks):
                    bank = (t % slots) * banks + c // 4
                    ins = pe.transpose(m.psum[0:width, bank, (c % 4) * P:(c % 4 + 1) * P],
                                       source(t, c), ident)
                ins.then_inc(m.products.sem, 1)

        def pieces(t):
            full = len([w for w in chunks if w == P])
            spans = [(c, min(c + 4, full), P) for c in range(0, full, 4)]
            spans += [(c, c + 1, chunks[c]) for c in range(full, len(chunks))]
            for a, b, rows in spans:
                bank = (t % slots) * banks + a // 4
                view = m.psum[0:rows, bank, (a % 4) * P:(a % 4 + b - a) * P]
                yield a, b, rows, view.rearrange("p (c q) -> p c q", q=P)

        @block.scalar
        def _(act):
            for t in range(TT):
                act.wait_ge(m.products.sem, m.products.at(t + 1))
                for a, b, rows, view in pieces(t):
                    ins = act.activation(high[0:rows, a:b, t * P:(t + 1) * P], view, ACT.Copy)
                ins.then_inc(m.high_done.sem, 1)

        @block.vector
        def _(dve):
            for t in range(TT):
                dve.wait_ge(m.high_done.sem, m.high_done.at(t + 1))
                for a, b, rows, view in pieces(t):
                    ins = dve.tensor_tensor(low[0:rows, a:b, t * P:(t + 1) * P], view,
                                            high[0:rows, a:b, t * P:(t + 1) * P], ALU.subtract)
                ins.then_inc(m.low_done.sem, 1)

    m.products.close(TT)
    m.high_done.close(TT)
    m.low_done.close(TT)


def project_transposed(m, w, x, out, n_out, n_tok, bias=None):
    groups = [(c, h) for c in range(n_out) for h in range(n_tok // BANK)]
    with m.block() as block:
        @block.tensor
        def _(pe):
            for g, (c, h) in enumerate(groups):
                if g >= 8:
                    pe.wait_ge(m.low_done.sem, m.low_done.at(g - 7))
                for k in range(KC):
                    ins = three_terms(pe, m.psum[:, g % 8, :],
                                      w[0][:, k, c * P:(c + 1) * P], w[1][:, k, c * P:(c + 1) * P],
                                      x[0][:, k, h * BANK:(h + 1) * BANK],
                                      x[1][:, k, h * BANK:(h + 1) * BANK], k == 0, k == KC - 1)
                ins.then_inc(m.products.sem, 1)

        @block.scalar
        def _(act):
            for g, (c, h) in enumerate(groups):
                act.wait_ge(m.products.sem, m.products.at(g + 1))
                dst = out[0][:, c, h * BANK:(h + 1) * BANK]
                if bias is None:
                    ins = act.activation(dst, m.psum[:, g % 8, :], ACT.Copy)
                else:
                    ins = act.activation(dst, m.psum[:, g % 8, :], ACT.Identity, bias=bias[:, c:c + 1])
                ins.then_inc(m.high_done.sem, 1)

        @block.vector
        def _(dve):
            for g, (c, h) in enumerate(groups):
                dve.wait_ge(m.high_done.sem, m.high_done.at(g + 1))
                hi = out[0][:, c, h * BANK:(h + 1) * BANK]
                lo = out[1][:, c, h * BANK:(h + 1) * BANK]
                if bias is None:
                    ins = dve.tensor_tensor(lo, m.psum[:, g % 8, :], hi, ALU.subtract)
                else:
                    ins = dve.scalar_tensor_tensor(lo, m.psum[:, g % 8, :], bias[:, c:c + 1], hi,
                                                   ALU.add, ALU.subtract)
                ins.then_inc(m.low_done.sem, 1)

    m.products.close(len(groups))
    m.high_done.close(len(groups))
    m.low_done.close(len(groups))


def project_values(m, w, x, values, n_tiles, heads, dh, ones_row=None, bias_row=None):
    per_entry = n_tiles // B
    width = heads * dh
    with m.block() as block:
        @block.gpsimd
        def _(pool):
            m.pchain.step(pool, pool.memset(values[:, :, :, :, dh:dh + 1], 1.0))

        @block.tensor
        def _(pe):
            for t in range(n_tiles):
                if t >= 8:
                    pe.wait_ge(m.low_done.sem, m.low_done.at(t - 7))
                out = m.psum[:, t % 8, 0:width]
                for k in range(KC):
                    ins = three_terms(pe, out, x[0][:, k, t * P:(t + 1) * P],
                                      x[1][:, k, t * P:(t + 1) * P], w[0][:, k, :], w[1][:, k, :],
                                      k == 0, k == KC - 1 and bias_row is None)
                if bias_row is not None:
                    ins = pe.matmul(out, ones_row, bias_row, start=False, stop=True)
                ins.then_inc(m.products.sem, 1)

        @block.scalar
        def _(act):
            for t in range(n_tiles):
                act.wait_ge(m.products.sem, m.products.at(t + 1))
                act.activation(values[:, t // per_entry, :, t % per_entry, 0:dh],
                               m.psum[:, t % 8, 0:width].rearrange("p (h d) -> p h d", d=dh),
                               ACT.Copy).then_inc(m.high_done.sem, 1)

        @block.vector
        def _(dve):
            for t in range(n_tiles):
                dve.wait_ge(m.high_done.sem, m.high_done.at(t + 1))
                dve.tensor_tensor(values[:, t // per_entry, :, t % per_entry, dh + 1:2 * dh + 1],
                                  m.psum[:, t % 8, 0:width].rearrange("p (h d) -> p h d", d=dh),
                                  values[:, t // per_entry, :, t % per_entry, 0:dh],
                                  ALU.subtract).then_inc(m.low_done.sem, 1)

    m.products.close(n_tiles)
    m.high_done.close(n_tiles)
    m.low_done.close(n_tiles)


def project_tokens(m, w, x, rows, n, finish, ones_row=None, bias_row=None):
    with m.block() as block:
        @block.tensor
        def _(pe):
            for t in range(TT):
                out = m.psum[:, t, 0:n]
                for k, r in enumerate(rows):
                    ins = three_terms(pe, out, x[0][0:r, k, t * P:(t + 1) * P],
                                      x[1][0:r, k, t * P:(t + 1) * P], w[0][0:r, k, :], w[1][0:r, k, :],
                                      k == 0, k == len(rows) - 1 and bias_row is None)
                if bias_row is not None:
                    ins = pe.matmul(out, ones_row, bias_row, start=False, stop=True)
                ins.then_inc(m.products.sem, 1)

        @block.vector
        def _(dve):
            for t in range(TT):
                dve.wait_ge(m.products.sem, m.products.at(t + 1))
                finish(dve, t, m.psum[:, t, 0:n])

    m.products.close(TT)


def store_heads(m, parts, scratch, n_tok):
    with m.block() as block:
        @block.sync
        def _(sp):
            n = 0
            for s in range(2):
                for b in range(B):
                    rows = parts[s].shape[1] * P
                    sp.dma_start(
                        scratch[s, b * rows:(b + 1) * rows, :].rearrange("(c p) q -> p c q", p=P),
                        parts[s][:, :, b * n_tok:(b + 1) * n_tok]).then_inc(m.stored.sem, 16)
                    n += 1
            sp.wait_ge(m.stored.sem, m.stored.at(16 * n))

    m.stored.close(16 * 2 * B)


def attention(m, ident, q_scr, k_scr, values, result, n_keys, heads, dh, mask_scr=None):
    nc = m.nc
    pairs = B * heads
    units = pairs * QT
    halves = n_keys // BANK
    tiles = n_keys // P
    scale = float(dh) ** -0.5
    narrow = dh == 16
    out_w = 2 * dh + 1 if narrow else dh + 1
    one = dh if narrow else dh
    rows = 3 * dh if narrow else 2 * dh
    loads = (6 if narrow else 5) + (mask_scr is not None)
    with ExitStack() as mem:
        def sb(name, shape, dt):
            return mem.enter_context(nc.sbuf_tensor(f"{name}_{nc.next_id()}", shape, dt))

        q_buf = sb("q_buf", [P, 2, NQ], F16)
        k_buf = sb("k_buf", [P, 2, n_keys], F16)
        kl_buf = None if narrow else sb("kl_buf", [P, 2, n_keys], F16)
        mask_buf = sb("mask_buf", [3, 2, n_keys], BF16) if mask_scr is not None else None
        ones3 = sb("ones3", [3, P], BF16) if mask_scr is not None else None
        probs = sb("probs", [P, 2, n_keys], F32)
        pt_hi = sb("pt_hi", [P, 2, tiles, P], F16)
        pt_lo = sb("pt_lo", [P, 2, tiles, P], F16)
        neg_max = sb("neg_max", [P, 4], F32)
        shift = sb("shift", [P, 4], F32)
        recip = sb("recip", [P, 2, QT], F32)
        part = sb("part", [P, 2, QT, dh], F32)

        def score_bank(u, h):
            return m.psum[:, (u % 2) * 2 + h, :]

        def turn_bank(u, h):
            return m.psum[:, 4 + (u * halves + h) % 2, :]

        def out_bank(head):
            return m.psum[:, 6 + head % 2, 0:QT * out_w].rearrange("p (t w) -> p t w", w=out_w)

        def pe_step(pe, base, k, pair):
            first = isinstance(base, int) and base + k
            if not (isinstance(base, int) and base + k + 3 >= units):
                u = k + 3
                if u % QT == 0:
                    head = u // QT
                    pe.wait_ge(m.operands[head % 2].sem,
                               m.operands[head % 2].at(0) + 16 * loads * (pair(2 * (head // 2)) // 2 + 1)
                               if isinstance(base, int) else
                               m.operands[head % 2].at(0) + loaded_at(base, head))
                if not (isinstance(base, int) and base + u < 2):
                    pe.wait_ge(m.probs.sem, m.probs.at(base + (u - 1)))
                par = (u // QT) % 2
                t = u % QT
                for h in range(halves):
                    out = score_bank(u, h)
                    cols = slice(h * BANK, (h + 1) * BANK)
                    ins = pe.matmul(out, q_buf[0:rows, par, t * P:(t + 1) * P],
                                    k_buf[0:rows, par, cols], start=True,
                                    stop=narrow and mask_scr is None)
                    if not narrow:
                        ins = pe.matmul(out, q_buf[0:dh, par, t * P:(t + 1) * P],
                                        kl_buf[0:dh, par, cols], start=False, stop=True)
                    if mask_scr is not None:
                        ins = pe.matmul(out, ones3[:, :], mask_buf[:, par, cols], start=False, stop=True)
                ins.then_inc(m.scores.sem, 1)
            if not (isinstance(base, int) and (base + k + 1 < 0 or base + k + 1 >= units)):
                u = k + 1
                pe.wait_ge(m.probs.sem, m.probs.at(base + (u + 1)))
                for h in range(halves):
                    if not (isinstance(base, int) and (base + u) * halves + h < 2):
                        pe.wait_ge(m.low_done.sem, m.low_done.at(base * halves + (u * halves + h - 1)))
                    for j in range(BANK // P):
                        ins = pe.transpose(turn_bank(u, h)[:, j * P:(j + 1) * P],
                                           probs[:, u % 2, h * BANK + j * P:h * BANK + (j + 1) * P],
                                           ident)
                    ins.then_inc(m.probs_t.sem, 1)
            if not (isinstance(base, int) and base + k < 0):
                u = k
                t = u % QT
                head = u // QT
                if t == 0:
                    pe.wait_ge(m.finished.sem, m.finished.at(pair(head)))
                pe.wait_ge(m.low_done.sem, m.low_done.at(base * halves + (u + 1) * halves))
                out = out_bank(head)[:, t, :]
                for j in range(tiles):
                    hi, lo = pt_hi[:, u % 2, j, :], pt_lo[:, u % 2, j, :]
                    v = values_of(pair(head), j)
                    if narrow:
                        pe.matmul(out, hi, v(0, out_w), start=j == 0, stop=False)
                        ins = pe.matmul(out[:, 0:dh + 1], lo, v(0, dh + 1), start=False,
                                        stop=j == tiles - 1)
                    else:
                        pe.matmul(out, hi, v(0, dh + 1), start=j == 0, stop=False)
                        pe.matmul(out[:, 0:dh], hi, v(dh + 1, 2 * dh + 1), start=False, stop=False)
                        ins = pe.matmul(out, lo, v(0, dh + 1), start=False, stop=j == tiles - 1)
                ins.then_inc(m.weighted.sem, 1)

        vw = 2 * dh + 1
        flat = values[:, :, :, :, :].rearrange("p b h t w -> p (b h t w)")

        def values_of(i, j):
            def cols(a, b):
                at = i * (tiles * vw) + (j * vw + a)
                return flat[:, bass.ds(at, b - a)] if not isinstance(at, int) else flat[:, at:at + b - a]
            return cols

        def loaded_at(base, head):
            return (base // 8 + (head // 2 + 1)) * (16 * loads)

        def act_step(act, base, k):
            if not (isinstance(base, int) and (base + k + 2 < 0 or base + k + 2 >= units)):
                u = k + 2
                act.wait_ge(m.maxima.sem, m.maxima.at(base + (u + 1)))
                if not (isinstance(base, int) and base + u < 2):
                    act.wait_ge(m.probs_t.sem, m.probs_t.at(base * halves + (u - 1) * halves))
                act.activation(probs[:, u % 2, :], m.psum[:, (u % 2) * 2:(u % 2) * 2 + halves, :]
                               .rearrange("p h q -> p (h q)"), ACT.Exp, bias=shift[:, u % 4:u % 4 + 1],
                               scale=scale).then_inc(m.probs.sem, 1)
            if not (isinstance(base, int) and (base + k + 1 < 0 or base + k + 1 >= units)):
                u = k + 1
                for h in range(halves):
                    act.wait_ge(m.probs_t.sem, m.probs_t.at(base * halves + (u * halves + h + 1)))
                    if h == 0 and not (isinstance(base, int) and base + u < 2):
                        act.wait_ge(m.weighted.sem, m.weighted.at(base + (u - 1)))
                    act.activation(pt_hi[:, u % 2, h * 4:(h + 1) * 4, :],
                                   turn_bank(u, h).rearrange("p (j q) -> p j q", q=P),
                                   ACT.Copy).then_inc(m.high_done.sem, 1)

        def dve_step(dve, base, k, pair):
            if not (isinstance(base, int) and base + k < 0):
                u = k
                for h in range(halves):
                    dve.wait_ge(m.high_done.sem, m.high_done.at(base * halves + (u * halves + h + 1)))
                    dve.tensor_tensor(pt_lo[:, u % 2, h * 4:(h + 1) * 4, :],
                                      turn_bank(u, h).rearrange("p (j q) -> p j q", q=P),
                                      pt_hi[:, u % 2, h * 4:(h + 1) * 4, :],
                                      ALU.subtract).then_inc(m.low_done.sem, 1)
            if not (isinstance(base, int) and base + k + 3 >= units):
                u = k + 3
                dve.wait_ge(m.scores.sem, m.scores.at(base + (u + 1)))
                m.vchain.step(dve, dve.tensor_reduce(
                    neg_max[:, u % 4:u % 4 + 1], m.psum[:, (u % 2) * 2:(u % 2) * 2 + halves, :],
                    AX.XY, ALU.max, negate=True))
                dve.tensor_scalar(shift[:, u % 4:u % 4 + 1], neg_max[:, u % 4:u % 4 + 1], scale,
                                  LN_P_SCALE, ALU.mult, ALU.add).then_inc(m.maxima.sem, 1)
            if k % QT == 1 and not (isinstance(base, int) and base + k < QT):
                normalise(dve, base, k // QT - 1, pair)

        def normalise(dve, base, head, pair):
            dve.wait_ge(m.weighted.sem, m.weighted.at(base + (head + 1) * QT))
            out = out_bank(head)
            r = recip[:, head % 2, :]
            m.vchain.step(dve, dve.reciprocal(r, out[:, :, one]))
            rb = r.unsqueeze(2).to_broadcast([P, QT, dh])
            i = pair(head)
            dst = result[:, :, i, :] if isinstance(i, int) else \
                result[:, :, bass.ds(i, 1), :].rearrange("p t o d -> p t (o d)")
            if narrow:
                m.vchain.step(dve, dve.tensor_tensor(part[:, 0, :, :], out[:, :, 0:dh], rb, ALU.mult))
                m.vchain.step(dve, dve.tensor_tensor(part[:, 1, :, :], out[:, :, dh + 1:2 * dh + 1], rb,
                                                     ALU.mult))
                dve.tensor_tensor(dst, part[:, 0, :, :], part[:, 1, :, :], ALU.add)\
                   .then_inc(m.finished.sem, 1)
            else:
                dve.tensor_tensor(dst, out[:, :, 0:dh], rb, ALU.mult).then_inc(m.finished.sem, 1)

        fin_steps = 3 if narrow else 1
        rounds = units // 8

        with m.block() as block:
            def load(sp, i, par):
                sem = m.operands[par].sem
                rq = lambda s: q_scr[s, bass.ds(i * dh, dh), :]
                rk = lambda s: k_scr[s, bass.ds(i * dh, dh), :]
                for s, at in (((0, 0), (1, 1), (0, 2)) if narrow else ((0, 0), (1, 1))):
                    sp.dma_start(q_buf[at * dh:(at + 1) * dh, par, :], rq(s)).then_inc(sem, 16)
                for s, at in (((0, 0), (0, 1), (1, 2)) if narrow else ((0, 0), (0, 1))):
                    sp.dma_start(k_buf[at * dh:(at + 1) * dh, par, :], rk(s)).then_inc(sem, 16)
                if not narrow:
                    sp.dma_start(kl_buf[0:dh, par, :], rk(1)).then_inc(sem, 16)
                if mask_scr is not None:
                    sp.dma_start(mask_buf[:, par, :], mask_scr[bass.ds(i, 1), :, :]
                                 .rearrange("o r k -> (o r) k")).then_inc(sem, 16)

            @block.sync
            def _(sp):
                load(sp, 0, 0)
                load(sp, 1, 1)
                with sp.Fori(0, pairs // 2 - 1) as j:
                    for par in range(2):
                        sp.wait_ge(m.scores.sem, m.scores.at(j * 8 + 4 * (par + 1)))
                        load(sp, j * 2 + (2 + par), par)

            @block.tensor
            def _(pe):
                def static_pair(base):
                    return lambda head: base // QT + head
                if mask_scr is not None:
                    pe.wait_ge(m.ready.sem, m.ready.at(1))
                for k in range(-3, 0):
                    pe_step(pe, 0, k, static_pair(0))
                with pe.Fori(0, rounds - 1) as j:
                    for k in range(8):
                        pe_step(pe, j * 8, k, lambda head: j * 2 + head)
                for k in range(8):
                    pe_step(pe, 8 * (rounds - 1), k, static_pair(8 * (rounds - 1)))

            @block.scalar
            def _(act):
                for k in range(-3, 0):
                    act_step(act, 0, k)
                with act.Fori(0, rounds - 1) as j:
                    for k in range(8):
                        act_step(act, j * 8, k)
                for k in range(8):
                    act_step(act, 8 * (rounds - 1), k)

            @block.vector
            def _(dve):
                dve.sem_inc(m.finished.sem, 1)
                for k in range(-3, 0):
                    dve_step(dve, 0, k, lambda head: head)
                for k in range(8):
                    dve_step(dve, 0, k, lambda head: head)
                with dve.Fori(0, rounds - 2) as r, m.vchain.loop(r, 8 + 2 * fin_steps, rounds - 2):
                    for k in range(8):
                        dve_step(dve, r * 8 + 8, k, lambda head: r * 2 + (head + 2))
                last = 8 * (rounds - 1)
                for k in range(8):
                    dve_step(dve, last, k, lambda head: last // QT + head)
                normalise(dve, last, 1, lambda head: last // QT + head)

            if mask_scr is not None:
                @block.gpsimd
                def _(pool):
                    pool.memset(ones3[:, :], 1.0).then_inc(m.ready.sem, 1)

    if mask_scr is not None:
        m.ready.close(1)
    for par in range(2):
        m.operands[par].close(16 * loads * (pairs // 2))
    m.scores.close(units)
    m.maxima.close(units)
    m.probs.close(units)
    m.probs_t.close(units * halves)
    m.high_done.close(units * halves)
    m.low_done.close(units * halves)
    m.weighted.close(units)
    m.finished.close(pairs + 1)


def quantise(m, tmp, src, dst, n_blocks):
    rows = src.shape[0]
    size = n_blocks * FP4_BLOCK
    amax, inv = tmp["amax"][0:rows, 0:n_blocks], tmp["inv"][0:rows, 0:n_blocks]
    xn, mag, spl, fine = (tmp["quant"][0:rows, j, 0:size] for j in range(4))

    def blocks(a):
        return a.rearrange("p (n b) -> p n b", b=FP4_BLOCK)

    def program(dve):
        step = m.vchain.step
        step(dve, dve.tensor_reduce(amax, src, AX.X, ALU.max, apply_absolute_value=True))
        step(dve, dve.tensor_scalar(amax, amax, 1.0 / 6.0, 1e-12, ALU.mult, ALU.max))
        step(dve, dve.reciprocal(inv, amax))
        step(dve, dve.tensor_scalar(inv, inv, TIE_DOWN, None, ALU.mult))
        step(dve, dve.tensor_tensor(blocks(xn), src, inv.unsqueeze(2).to_broadcast([rows, n_blocks, FP4_BLOCK]),
                                    ALU.mult))
        step(dve, dve.tensor_scalar(mag.bitcast(U32), xn.bitcast(U32), 0x7FFFFFFF, None,
                                    ALU.bitwise_and))
        step(dve, dve.tensor_scalar(fine, mag, 1.0, HALF_GRID, ALU.min, ALU.add))
        step(dve, dve.tensor_scalar(mag, mag, 1.0, None, ALU.max))
        step(dve, dve.scalar_tensor_tensor(spl, mag, SPLIT_TWO_BITS, mag, ALU.mult, ALU.subtract))
        step(dve, dve.scalar_tensor_tensor(spl, mag, SPLIT_TWO_BITS, spl, ALU.mult, ALU.subtract))
        step(dve, dve.scalar_tensor_tensor(mag, fine, HALF_GRID + 1.0, spl, ALU.subtract, ALU.add))
        step(dve, dve.tensor_scalar(xn.bitcast(U32), xn.bitcast(U32), 0x80000000, None, ALU.bitwise_and))
        step(dve, dve.tensor_tensor(mag.bitcast(U32), mag.bitcast(U32), xn.bitcast(U32), ALU.bitwise_or))
        step(dve, dve.tensor_tensor(dst, blocks(mag),
                                    amax.unsqueeze(2).to_broadcast([rows, n_blocks, FP4_BLOCK]), ALU.mult))
    return program


def feed_forward_gelu(m, w, x, out, bias, n_out):
    groups = [(c, h) for c in range(n_out) for h in range(T // BANK)]
    nc = m.nc
    with nc.sbuf_tensor("gelu_out", [P, 2, BANK], F32) as full, m.block() as block:
        @block.tensor
        def _(pe):
            for g, (c, h) in enumerate(groups):
                if g >= 8:
                    pe.wait_ge(m.act_ready.sem, m.act_ready.at(g - 7))
                for k in range(KC):
                    ins = three_terms(pe, m.psum[:, g % 8, :],
                                      w[0][:, k, c * P:(c + 1) * P], w[1][:, k, c * P:(c + 1) * P],
                                      x[0][:, k, h * BANK:(h + 1) * BANK],
                                      x[1][:, k, h * BANK:(h + 1) * BANK], k == 0, k == KC - 1)
                ins.then_inc(m.products.sem, 1)

        @block.scalar
        def _(act):
            for g, (c, h) in enumerate(groups):
                act.wait_ge(m.products.sem, m.products.at(g + 1))
                if g >= 2:
                    act.wait_ge(m.low_done.sem, m.low_done.at(g - 1))
                act.activation(full[:, g % 2, :], m.psum[:, g % 8, :], ACT.Gelu,
                               bias=bias[:, c:c + 1]).then_inc(m.act_ready.sem, 1)

        @block.vector
        def _(dve):
            for g, (c, h) in enumerate(groups):
                hi = out[0][:, c, h * BANK:(h + 1) * BANK]
                dve.wait_ge(m.act_ready.sem, m.act_ready.at(g + 1))
                m.vchain.step(dve, dve.tensor_copy(hi, full[:, g % 2, :]))
                dve.tensor_tensor(out[1][:, c, h * BANK:(h + 1) * BANK], full[:, g % 2, :], hi,
                                  ALU.subtract).then_inc(m.low_done.sem, 1)

    m.products.close(len(groups))
    m.act_ready.close(len(groups))
    m.low_done.close(len(groups))


FFN_H = 704
FFN_BLOCKS = FFN_H // FP4_BLOCK
FFN_ROWS = [P] * (FFN_H // P) + [FFN_H % P]
MOE_H = 682
MOE_ROWS = [P] * (MOE_H // P) + [MOE_H % P]
MOE_CH = len(MOE_ROWS)
EXPERTS, TOP = 8, 4
SLOTS = EXPERTS + 1


def gate_up(m, x, wg, wu, hid):
    half = FFN_H // 2
    with m.nc.sbuf_tensor("silu_out", [P, 2, 2, half], F32) as silu, m.block() as block:
        @block.tensor
        def _(pe):
            for t in range(TT):
                if t >= 2:
                    pe.wait_ge(m.low_done.sem, m.low_done.at(t - 1))
                for a, w in enumerate((wg, wu)):
                    for s in range(2):
                        out = m.psum[:, (t % 2) * 4 + 2 * a + s, 0:half]
                        for k in range(KC):
                            ins = three_terms(pe, out, x[0][:, k, t * P:(t + 1) * P],
                                              x[1][:, k, t * P:(t + 1) * P],
                                              w[0][:, k, s * half:(s + 1) * half],
                                              w[1][:, k, s * half:(s + 1) * half], k == 0, k == KC - 1)
                    ins.then_inc(m.products.sem, 1)

        @block.scalar
        def _(act):
            for t in range(TT):
                act.wait_ge(m.products.sem, m.products.at(2 * t + 1))
                if t >= 2:
                    act.wait_ge(m.low_done.sem, m.low_done.at(t - 1))
                act.activation(silu[:, t % 2, :, :], m.psum[:, (t % 2) * 4:(t % 2) * 4 + 2, 0:half],
                               ACT.Silu).then_inc(m.act_ready.sem, 1)

        @block.vector
        def _(dve):
            for t in range(TT):
                dve.wait_ge(m.act_ready.sem, m.act_ready.at(t + 1))
                dve.wait_ge(m.products.sem, m.products.at(2 * t + 2))
                dve.tensor_tensor(hid[:, t, :].rearrange("p (s q) -> p s q", s=2),
                                  m.psum[:, (t % 2) * 4 + 2:(t % 2) * 4 + 4, 0:half],
                                  silu[:, t % 2, :, :], ALU.mult).then_inc(m.low_done.sem, 1)

    m.products.close(2 * TT)
    m.act_ready.close(TT)
    m.low_done.close(TT)


def route(m, tmp, gate, weights):
    nc = m.nc
    with ExitStack() as mem:
        beats = mem.enter_context(nc.sbuf_tensor("beats", [P, TT, EXPERTS, EXPERTS], F32))
        rank = mem.enter_context(nc.sbuf_tensor("rank", [P, TT, EXPERTS], F32))
        top = mem.enter_context(nc.sbuf_tensor("top", [P, TT], F32))
        with m.block() as block:
            @block.vector
            def _(dve):
                step = m.vchain.step
                step(dve, dve.memset(weights[:, 0, :], 1.0))
                for e in range(EXPERTS):
                    mine = gate[:, :, e:e + 1].to_broadcast([P, TT, EXPERTS])
                    if e:
                        step(dve, dve.tensor_tensor(beats[:, :, e, 0:e], gate[:, :, 0:e], mine[:, :, 0:e],
                                                    ALU.is_ge))
                    step(dve, dve.tensor_tensor(beats[:, :, e, e:EXPERTS], gate[:, :, e:EXPERTS],
                                                mine[:, :, e:EXPERTS], ALU.is_gt))
                step(dve, dve.tensor_reduce(rank[:, :, :], beats[:, :, :, :], AX.X, ALU.add))
                step(dve, dve.tensor_scalar(rank[:, :, :], rank[:, :, :], float(TOP), None, ALU.is_lt))
                step(dve, dve.tensor_reduce(top[:, :], gate[:, :, :], AX.X, ALU.max))
                step(dve, dve.tensor_tensor(gate[:, :, :], gate[:, :, :],
                                            top[:, :].unsqueeze(2).to_broadcast([P, TT, EXPERTS]),
                                            ALU.subtract))
                dve.nop().then_inc(m.ready.sem, 1)
                dve.wait_ge(m.act_ready.sem, m.act_ready.at(1))
                step(dve, dve.tensor_tensor(gate[:, :, :], gate[:, :, :], rank[:, :, :], ALU.mult))
                step(dve, dve.tensor_reduce(top[:, :], gate[:, :, :], AX.X, ALU.add))
                step(dve, dve.reciprocal(top[:, :], top[:, :]))
                step(dve, dve.tensor_tensor(weights[:, 1:SLOTS, :].rearrange("p e t -> p t e"),
                                            gate[:, :, :],
                                            top[:, :].unsqueeze(2).to_broadcast([P, TT, EXPERTS]),
                                            ALU.mult))

            @block.scalar
            def _(act):
                act.wait_ge(m.ready.sem, m.ready.at(1))
                act.activation(gate[:, :, :], gate[:, :, :], ACT.Exp).then_inc(m.act_ready.sem, 1)

    m.ready.close(1)
    m.act_ready.close(1)


def mixture(m, x, w12_dram, w3_dram, weights, acc):
    nc = m.nc
    per = MOE_CH * 2
    with ExitStack() as mem:
        def sb(name, shape, dt):
            return mem.enter_context(nc.sbuf_tensor(name, shape, dt))

        w12 = sb("w12", [P, KC * 2 * MOE_H], F32)
        w3 = sb("w3", [P, MOE_CH, D], F32)
        w12_hi = sb("w12_hi", [P, KC, 2, MOE_H], F16)
        w12_lo = sb("w12_lo", [P, KC, 2, MOE_H], F16)
        w3_hi = sb("w3_hi", [P, MOE_CH, D], F16)
        w3_lo = sb("w3_lo", [P, MOE_CH, D], F16)
        silu = sb("silu", [P, 2, BANK], F32)
        prod = sb("prod", [P, 2, BANK], F32)
        g_hi = sb("g_hi", [P, MOE_CH, T], F16)
        g_lo = sb("g_lo", [P, MOE_CH, T], F16)
        last = SLOTS - 1
        full = MOE_H // P
        tail = MOE_ROWS[-1]

        def up_banks(u):
            return m.psum[:, 2 * (u % 2), :], m.psum[:, 2 * (u % 2) + 1, :]

        def split_w12_high(act, e):
            act.wait_ge(m.w12_loaded.sem, m.w12_loaded.at(e * 16 + 16))
            act.wait_ge(m.products.sem, m.products.at(e * (2 * per)))
            act.activation(w12_hi[:, :, :, :].rearrange("p k w n -> p (k w n)"), w12[:, :],
                           ACT.Copy).then_inc(m.w12_high.sem, 1)

        def split_w12_low(dve, e):
            dve.wait_ge(m.w12_high.sem, m.w12_high.at(e + 1))
            dve.tensor_tensor(w12_lo[:, :, :, :].rearrange("p k w n -> p (k w n)"), w12[:, :],
                              w12_hi[:, :, :, :].rearrange("p k w n -> p (k w n)"),
                              ALU.subtract).then_inc(m.w12_low.sem, 1)

        with m.block() as block:
            @block.sync
            def _(sp):
                with sp.Fori(0, SLOTS) as e:
                    sp.wait_ge(m.w12_low.sem, m.w12_low.at(e))
                    sp.dma_start(w12[:, :], w12_dram[bass.ds(e, 1), :, :].rearrange("o p n -> (o p) n"))\
                      .then_inc(m.w12_loaded.sem, 16)
                    sp.wait_ge(m.w3_low.sem, m.w3_low.at(e))
                    rows = w3_dram[bass.ds(e, 1), :, :].rearrange("o h d -> (o h) d")
                    sp.dma_start(w3[:, 0:full, :], rows[0:full * P, :].rearrange("(c p) d -> p c d", p=P))\
                      .then_inc(m.w3_loaded.sem, 16)
                    sp.dma_start(w3[0:tail, full, :], rows[full * P:MOE_H, :])\
                      .then_inc(m.w3_loaded.sem, 16)

            @block.tensor
            def _(pe):
                with pe.Fori(0, SLOTS) as e:
                    pe.wait_ge(m.w12_low.sem, m.w12_low.at(e + 1))
                    for u in range(per):
                        half, c = divmod(u, MOE_CH)
                        r = MOE_ROWS[c]
                        if u >= 2:
                            pe.wait_ge(m.evacuated.sem, m.evacuated.at(e * per + (u - 1)))
                        else:
                            pe.wait_ge(m.evacuated.sem, m.evacuated.at(e * per))
                        for a in range(2):
                            out = up_banks(u)[a][0:r, :]
                            for k in range(KC):
                                ins = three_terms(pe, out, w12_hi[:, k, a, c * P:c * P + r],
                                                  w12_lo[:, k, a, c * P:c * P + r],
                                                  x[0][:, k, half * BANK:(half + 1) * BANK],
                                                  x[1][:, k, half * BANK:(half + 1) * BANK],
                                                  k == 0, k == KC - 1)
                            ins.then_inc(m.products.sem, 1)
                    pe.wait_ge(m.w3_low.sem, m.w3_low.at(e + 1))
                    for t in range(TT):
                        if t % (TT // 2) == 0:
                            pe.wait_ge(m.low_done.sem, m.low_done.at(e * per + (t // (TT // 2) + 1) * MOE_CH))
                        if t >= 4:
                            pe.wait_ge(m.down_done.sem, m.down_done.at(e * TT + (t - 3)))
                        else:
                            pe.wait_ge(m.down_done.sem, m.down_done.at(e * TT))
                        out = m.psum[:, 4 + t % 4, 0:D]
                        for c, r in enumerate(MOE_ROWS):
                            ins = three_terms(pe, out, g_hi[0:r, c, t * P:(t + 1) * P],
                                              g_lo[0:r, c, t * P:(t + 1) * P],
                                              w3_hi[0:r, c, :], w3_lo[0:r, c, :], c == 0, c == MOE_CH - 1)
                        ins.then_inc(m.weighted.sem, 1)

            def act_expert(act, e, more):
                for u in range(per):
                    half, c = divmod(u, MOE_CH)
                    r = MOE_ROWS[c]
                    act.wait_ge(m.products.sem, m.products.at(e * (2 * per) + (2 * u + 1)))
                    act.wait_ge(m.evacuated.sem, m.evacuated.at(e * per + max(u - 1, 0)))
                    act.activation(silu[0:r, u % 2, :], up_banks(u)[0][0:r, :], ACT.Silu)\
                       .then_inc(m.act_ready.sem, 1)
                    act.wait_ge(m.evacuated.sem, m.evacuated.at(e * per + (u + 1)))
                    act.wait_ge(m.weighted.sem, m.weighted.at(e * TT))
                    act.activation(g_hi[0:r, c, half * BANK:(half + 1) * BANK], prod[0:r, u % 2, :],
                                   ACT.Copy).then_inc(m.high_done.sem, 1)
                    if u == 2:
                        act.wait_ge(m.w3_loaded.sem, m.w3_loaded.at(e * 32 + 32))
                        act.activation(w3_hi[:, 0:full, :], w3[:, 0:full, :], ACT.Copy)\
                           .then_inc(m.w3_high.sem, 1)
                        act.activation(w3_hi[0:tail, full, :], w3[0:tail, full, :], ACT.Copy)\
                           .then_inc(m.w3_high.sem, 1)
                if more:
                    split_w12_high(act, e + 1)

            @block.scalar
            def _(act):
                split_w12_high(act, 0)
                with act.Fori(0, last) as e:
                    act_expert(act, e, True)
                act_expert(act, last, False)

            def dve_expert(dve, e, more):
                for u in range(per):
                    half, c = divmod(u, MOE_CH)
                    r = MOE_ROWS[c]
                    dve.wait_ge(m.act_ready.sem, m.act_ready.at(e * per + (u + 1)))
                    dve.wait_ge(m.products.sem, m.products.at(e * (2 * per) + (2 * u + 2)))
                    dve.wait_ge(m.high_done.sem, m.high_done.at(e * per + max(u - 1, 0)))
                    dve.tensor_tensor(prod[0:r, u % 2, :], up_banks(u)[1][0:r, :], silu[0:r, u % 2, :],
                                      ALU.mult).then_inc(m.evacuated.sem, 1)
                    dve.wait_ge(m.high_done.sem, m.high_done.at(e * per + (u + 1)))
                    dve.tensor_tensor(g_lo[0:r, c, half * BANK:(half + 1) * BANK], prod[0:r, u % 2, :],
                                      g_hi[0:r, c, half * BANK:(half + 1) * BANK],
                                      ALU.subtract).then_inc(m.low_done.sem, 1)
                    if u == 2:
                        dve.wait_ge(m.w3_high.sem, m.w3_high.at(e * 2 + 2))
                        m.vchain.step(dve, dve.tensor_tensor(w3_lo[0:tail, full, :], w3[0:tail, full, :],
                                                             w3_hi[0:tail, full, :], ALU.subtract))
                        dve.tensor_tensor(w3_lo[:, 0:full, :], w3[:, 0:full, :], w3_hi[:, 0:full, :],
                                          ALU.subtract).then_inc(m.w3_low.sem, 1)
                if more:
                    split_w12_low(dve, e + 1)
                for t in range(TT):
                    dve.wait_ge(m.weighted.sem, m.weighted.at(e * TT + (t + 1)))
                    w = weights[:, e, t:t + 1] if isinstance(e, int) else \
                        weights[:, bass.ds(e, 1), t:t + 1].rearrange("p o t -> p (o t)")
                    dve.wait_ge(m.down_done.sem, m.down_done.at(e * TT + 0))
                    dve.scalar_tensor_tensor(acc[:, t, :], m.psum[:, 4 + t % 4, 0:D], w, acc[:, t, :],
                                             ALU.mult, ALU.add).then_inc(m.down_done.sem, 1)

            @block.vector
            def _(dve):
                m.vchain.step(dve, dve.memset(acc[:, :, :], 0.0))
                split_w12_low(dve, 0)
                with dve.Fori(0, last) as e, m.vchain.loop(e, 1, last):
                    dve_expert(dve, e, True)
                dve_expert(dve, last, False)

    m.w12_loaded.close(16 * SLOTS)
    m.w3_loaded.close(32 * SLOTS)
    m.w12_high.close(SLOTS)
    m.w12_low.close(SLOTS)
    m.w3_high.close(2 * SLOTS)
    m.w3_low.close(SLOTS)
    m.products.close(2 * per * SLOTS)
    m.act_ready.close(per * SLOTS)
    m.evacuated.close(per * SLOTS)
    m.high_done.close(per * SLOTS)
    m.low_done.close(per * SLOTS)
    m.weighted.close(TT * SLOTS)
    m.down_done.close(TT * SLOTS)


def flamingo_gated_kernel(nc, a, out, stop=99):
    ctx = ExitStack()
    with ctx:
        m = Machine(nc, ctx)

        used = {}

        def sb(name, shape, dt, scope=ctx):
            used[name] = used.get(name, 0) + 1
            return scope.enter_context(nc.sbuf_tensor(f"{name}_{used[name]}", shape, dt))

        ident = sb("ident", [P, P], F32)
        res = sb("res", [P, TT, D], F32)
        z = sb("z", [P, TT, D], F32)
        x_t = (sb("xt_hi", [P, KC, T], F16), sb("xt_lo", [P, KC, T], F16))
        tanh_g = sb("tanh_g", [P, 4], F32)
        ones_row = sb("ones_row", [1, P], F32)
        tmp = {"stats": sb("stats", [P, TT, 6], F32), "mv": sb("mv", [P, TT, 2], F32),
               "rstd": sb("rstd", [P, TT], F32)}
        dram = lambda name, shape, dt: nc.dram_tensor(name, shape, dt, kind="Internal").ap()
        q0_scr = dram("q0_scr", (2, B * D, NQ), F16)
        k0_scr = dram("k0_scr", (2, B * D, NCTX), F16)
        k1_scr = dram("k1_scr", (2, B * D, NQ), F16)
        D1 = 512
        q2_scr = dram("q2_scr", (2, B * D1, NQ), F16)
        k2_scr = dram("k2_scr", (2, B * D1, NCTX), F16)
        mask_scr = dram("mask_scr", (B * 16, 3, NCTX), BF16)

        def gated(i):
            def finish(dve, t, view):
                dve.scalar_tensor_tensor(res[:, t, :], view, tanh_g[:, i:i + 1], res[:, t, :],
                                         ALU.mult, ALU.add)
            return finish

        def add_residual(dve, t, view):
            dve.tensor_tensor(z[:, t, :], view, z[:, t, :], ALU.add)

        def load_all(items, extra=None):
            with m.block() as block:
                @block.sync
                def _(sp):
                    for dst, src in items:
                        sp.dma_start(dst, src).then_inc(m.loaded.sem, 16)
                    sp.wait_ge(m.loaded.sem, m.loaded.at(16 * len(items)))
            m.loaded.close(16 * len(items))

        def row(name):
            return a[name].rearrange("(o n) -> o n", o=1)

        def everywhere(name):
            return a[name].rearrange("(o n) -> o n", o=1).partition_broadcast(P) \
                if False else a[name].rearrange("(o n) -> o n", o=1).to_broadcast([P, a[name].shape[0]])

        def weight(name):
            return a[name].rearrange("(c p) n -> p c n", p=P)

        def column(name):
            return a[name + "_columns"]

        load_all([(ident[:, :], a["identity"]), (res[:, :, :], a["x"].rearrange("b (t p) d -> p (b t) d", p=P)),
                  (tanh_g[:, 0:2], everywhere("g_xattn")), (tanh_g[:, 2:4], everywhere("g_ffn"))])
        with m.block() as block:
            @block.scalar
            def _(act):
                act.activation(tanh_g[:, :], tanh_g[:, :], ACT.Tanh)

            @block.gpsimd
            def _(pool):
                m.pchain.step(pool, pool.memset(ones_row[:, :], 1.0))

        def token_source(t, c):
            return z[:, t, c * P:(c + 1) * P]

        def to_x_t():
            transpose_split(m, ident[:, :], token_source, [P] * KC, *(v[:, :, :] for v in x_t))

        x_views = tuple(v[:, :, :] for v in x_t)

        def pair_of(name, shape, scope):
            return tuple(sb(f"{name}_{s}", shape, F16, scope)[tuple([slice(None)] * len(shape))]
                         for s in ("hi", "lo"))

        def split_weights(names, kc, scope):
            outs = [pair_of(name, [P, kc, a[name].shape[1]], scope) for name in names]
            with ExitStack() as staging:
                items = []
                for name, (high, low) in zip(names, outs):
                    st = sb(f"{name}_f32", [P, kc, a[name].shape[1]], F32, staging)
                    items.append((st[:, :, :], weight(name), high, low))
                load_split(m, items)
            return outs

        layer_norm(m, tmp, res, z)
        to_x_t()
        with ExitStack() as s_ctx:
            result = sb("heads_out", [P, QT, B * 16, 16], F32, s_ctx)
            values = sb("values0", [P, B, 16, NCTX // P, 33], F16, s_ctx)
            with ExitStack() as scope:
                wq, wk, wv = split_weights(["L0_xattn_cq_w", "L0_xattn_ck_w", "L0_xattn_cv_w"], KC, scope)
                c_t = split_weights(["ctx_t"], KC, scope)[0]
                qb = sb("qb", [P, KC], F32, scope)
                kb = sb("kb", [P, KC], F32, scope)
                vb = sb("vb", [1, D], F32, scope)
                mask = sb("mask", [3, B * NCTX], F32, scope)
                part = sb("mask_part", [3, 3, B * NCTX], BF16, scope)
                load_all([(qb[:, :], column("L0_xattn_cq_b")), (kb[:, :], column("L0_xattn_ck_b")),
                          (vb[:, :], row("L0_xattn_cv_b"))] +
                         [(mask[r:r + 1, :], a["mask_Bx1x1xS2_ff0"].rearrange("b u v k -> (u v) (b k)"))
                          for r in range(3)])
                with m.block() as block:
                    @block.vector
                    def _(dve):
                        step = m.vchain.step
                        step(dve, dve.tensor_scalar(mask[:, :], mask[:, :], 4.0, None, ALU.mult))
                        for r in range(3):
                            step(dve, dve.tensor_copy(part[:, r, :], mask[:, :]))
                            step(dve, dve.tensor_tensor(mask[:, :], mask[:, :], part[:, r, :], ALU.subtract))
                with m.block() as block:
                    @block.sync
                    def _(sp):
                        for i in range(B * 16):
                            for r in range(3):
                                sp.dma_start(mask_scr[i, r:r + 1, :],
                                             part[r:r + 1, r, (i // 16) * NCTX:(i // 16 + 1) * NCTX])\
                                  .then_inc(m.stored.sem, 16)
                        sp.wait_ge(m.stored.sem, m.stored.at(16 * 3 * B * 16))
                m.stored.close(16 * 3 * B * 16)
                q_t = pair_of("q_t", [P, KC, T], scope)
                k_t = pair_of("k_t", [P, KC, B * NCTX], scope)
                project_transposed(m, wq, x_views, q_t, KC, T, qb)
                project_transposed(m, wk, c_t, k_t, KC, B * NCTX, kb)
                project_values(m, wv, c_t, values, B * NCTX // P, 16, 16, ones_row[:, :], vb[:, :])
                store_heads(m, q_t, q0_scr, NQ)
                store_heads(m, k_t, k0_scr, NCTX)
            if stop > 1:
                attention(m, ident[:, :], q0_scr, k0_scr, values, result, NCTX, 16, 16, mask_scr)

            def self_output(prefix, out_dst=z):
                with ExitStack() as scope:
                    w, = split_weights([prefix + "_w"], KC, scope)
                    b = sb(prefix + "_b", [1, D], F32, scope)
                    g = sb(prefix + "_g", [P, D], F32, scope)
                    be = sb(prefix + "_be", [P, D], F32, scope)
                    load_all([(b[:, :], row(prefix + "_b")), (g[:, :], everywhere(prefix + "_g")),
                              (be[:, :], everywhere(prefix + "_be"))])
                    project_tokens(m, w, x_views, [P] * KC, D, add_residual, ones_row[:, :], b[:, :])
                    layer_norm(m, tmp, z, z, g[:, :], be[:, :])

            def head_source(t, c):
                first = (t // QT) * 16 + 8 * c
                return result[:, t % QT, first:first + 8, :].rearrange("p h d -> p (h d)")

            if stop > 1:
                transpose_split(m, ident[:, :], head_source, [P] * KC, *x_views)
                self_output("L0_xattn_co")
            if stop > 2:
                to_x_t()
                values1 = sb("values1", [P, B, 16, NQ // P, 33], F16, s_ctx)
                with ExitStack() as scope:
                    wq, wk, wv = split_weights(["L0_xattn_sq_w", "L0_xattn_sk_w", "L0_xattn_sv_w"], KC, scope)
                    qb = sb("sqb", [P, KC], F32, scope)
                    kb = sb("skb", [P, KC], F32, scope)
                    vb = sb("svb", [1, D], F32, scope)
                    load_all([(qb[:, :], column("L0_xattn_sq_b")), (kb[:, :], column("L0_xattn_sk_b")),
                              (vb[:, :], row("L0_xattn_sv_b"))])
                    q_t = pair_of("sq_t", [P, KC, T], scope)
                    k_t = pair_of("sk_t", [P, KC, T], scope)
                    project_transposed(m, wq, x_views, q_t, KC, T, qb)
                    project_transposed(m, wk, x_views, k_t, KC, T, kb)
                    project_values(m, wv, x_views, values1, TT, 16, 16, ones_row[:, :], vb[:, :])
                    store_heads(m, q_t, q0_scr, NQ)
                    store_heads(m, k_t, k1_scr, NQ)
                attention(m, ident[:, :], q0_scr, k1_scr, values1, result, NQ, 16, 16)
                transpose_split(m, ident[:, :], head_source, [P] * KC, *x_views)
                self_output("L0_xattn_so")
        if stop > 3:
            to_x_t()
            with ExitStack() as scope:
                fi, = split_weights(["L0_xattn_fi_w"], KC, scope)
                fo, = split_weights(["L0_xattn_fo_w"], 8, scope)
                fib = sb("fib", [P, 8], F32, scope)
                b = sb("fob", [1, D], F32, scope)
                g = sb("fog", [P, D], F32, scope)
                be = sb("fobe", [P, D], F32, scope)
                load_all([(fib[:, :], column("L0_xattn_fi_b")), (b[:, :], row("L0_xattn_fo_b")),
                          (g[:, :], everywhere("L0_xattn_fo_g")), (be[:, :], everywhere("L0_xattn_fo_be"))])
                hid = pair_of("gelu", [P, 8, T], scope)
                feed_forward_gelu(m, fi, x_views, hid, fib, 8)
                project_tokens(m, fo, hid, [P] * 8, D, add_residual, ones_row[:, :], b[:, :])
                layer_norm(m, tmp, z, z, g[:, :], be[:, :])
            with m.block() as block:
                @block.vector
                def _(dve):
                    for t in range(TT):
                        dve.scalar_tensor_tensor(res[:, t, :], z[:, t, :], tanh_g[:, 0:1], res[:, t, :],
                                                 ALU.mult, ALU.add)
        if stop > 4:
            with ExitStack() as scope:
                quant_ctx = ExitStack()
                wg_t = pair_of("wg_t", [P, KC, FFN_H], scope)
                wu_t = pair_of("wu_t", [P, KC, FFN_H], scope)
                wd_t = pair_of("wd_t", [P, 6, D], scope)
                hid = sb("ffn_hid", [P, TT, FFN_H], F32, scope)
                tmp["amax"] = sb("amax", [P, 6 * D // 16], F32, scope)
                tmp["inv"] = sb("inv", [P, 6 * D // 16], F32, scope)
                tmp["quant"] = sb("quant", [P, 4, 6 * D], F32, scope)
                with ExitStack() as ws:
                    wg = sb("wg", [P, 6, D], F32, ws)
                    wu = sb("wu", [P, 6, D], F32, ws)
                    wd = sb("wd", [P, KC, FFN_H], F32, ws)
                    items = []
                    for dst, name in ((wg, "L0_ffn_w_gate"), (wu, "L0_ffn_w_up")):
                        items.append((dst[:, 0:5, :], a[name][0:640, :].rearrange("(c p) n -> p c n", p=P)))
                        items.append((dst[0:64, 5, :], a[name][640:704, :]))
                    items.append((wd[:, :, :], weight("L0_ffn_w_down")))
                    load_all(items)
                    views = []
                    for wt in (wg, wu):
                        views.append((wt[:, 0:5, :].rearrange("p c (n b) -> p (c n) b", b=16), 80))
                        views.append((wt[0:64, 5, :].rearrange("p (n b) -> p n b", b=16), 16))
                    for c in range(KC):
                        views.append((wd[:, c, :].rearrange("p (n b) -> p n b", b=16), FFN_BLOCKS))
                    with m.block() as block:
                        @block.vector
                        def _(dve):
                            for v, n in views:
                                quantise(m, tmp, v, v, n)(dve)
                    for wt, dst in ((wg, wg_t), (wu, wu_t)):
                        turn_weight(m, ident, wt, FFN_ROWS, KC, dst)
                    turn_weight(m, ident, wd, [P] * KC, 6, wd_t, FFN_ROWS)
                layer_norm(m, tmp, res, z)
                with m.block() as block:
                    @block.vector
                    def _(dve):
                        for t in range(0, TT, 4):
                            v = z[:, t:t + 4, :].rearrange("p t (n b) -> p (t n) b", b=16)
                            quantise(m, tmp, v, v, 64)(dve)
                to_x_t()
                gate_up(m, x_views, wg_t, wu_t, hid)
                with m.block() as block:
                    @block.vector
                    def _(dve):
                        for t in range(0, TT, 2):
                            v = hid[:, t:t + 2, :].rearrange("p t (n b) -> p (t n) b", b=16)
                            quantise(m, tmp, v, v, 2 * FFN_BLOCKS)(dve)
                h_t = pair_of("hid_t", [P, 6, T], scope)
                transpose_split(m, ident[:, :],
                                lambda t, c: hid[:, t, c * P:c * P + FFN_ROWS[c]], FFN_ROWS, *h_t)
                project_tokens(m, wd_t, h_t, FFN_ROWS, D, gated(2))
        if stop > 5:
            layer_norm(m, tmp, res, z)
            to_x_t()
            with ExitStack() as s_ctx:
                values = sb("values2", [P, B, 8, NCTX // P, 129], F16, s_ctx)
                result = sb("heads_out2", [P, QT, B * 8, 64], F32, s_ctx)
                with ExitStack() as scope:
                    c_t = split_weights(["ctx_t"], KC, scope)[0]
                    wq, = split_weights(["L1_xattn_Wq"], KC, scope)
                    with ExitStack() as s:
                        q_t = pair_of("q2_t", [P, 4, T], s)
                        project_transposed(m, wq, x_views, q_t, 4, T)
                        store_heads(m, q_t, q2_scr, NQ)
                    wk, = split_weights(["L1_xattn_Wk"], KC, scope)
                    with ExitStack() as s:
                        k_t = pair_of("k2_t", [P, 4, B * NCTX], s)
                        project_transposed(m, wk, c_t, k_t, 4, B * NCTX)
                        store_heads(m, k_t, k2_scr, NCTX)
                    wv, = split_weights(["L1_xattn_Wv"], KC, scope)
                    project_values(m, wv, c_t, values, B * NCTX // P, 8, 64)
                attention(m, ident[:, :], q2_scr, k2_scr, values, result, NCTX, 8, 64)
                with ExitStack() as scope:
                    a_t = pair_of("a2_t", [P, 4, T], scope)
                    transpose_split(m, ident[:, :],
                                    lambda t, c: result[:, t % QT, (t // QT) * 8 + 2 * c:
                                                        (t // QT) * 8 + 2 * c + 2, :]
                                    .rearrange("p h d -> p (h d)"), [P] * 4, *a_t)
                    wo, = split_weights(["L1_xattn_Wo"], 4, scope)
                    b = sb("bo", [1, D], F32, scope)
                    load_all([(b[:, :], row("L1_xattn_bo"))])
                    project_tokens(m, wo, a_t, [P] * 4, D, gated(1), ones_row[:, :], b[:, :])
        if stop > 6:
            layer_norm(m, tmp, res, z)
            to_x_t()
            with ExitStack() as scope:
                gate = sb("gate", [P, TT, EXPERTS], F32, scope)
                weights = sb("expert_weights", [P, SLOTS, TT], F32, scope)
                with ExitStack() as s:
                    wr, = split_weights(["L1_ffn_Wg_t"], KC, s)
                    rb = sb("rb", [1, EXPERTS], F32, s)
                    load_all([(rb[:, :], row("L1_ffn_routing_bias"))])

                    def keep_gate(dve, t, view):
                        dve.tensor_copy(gate[:, t, :], view)

                    project_tokens(m, wr, x_views, [P] * KC, EXPERTS, keep_gate, ones_row[:, :], rb[:, :])
                route(m, tmp, gate, weights)
                acc = sb("acc", [P, TT, D], F32, scope)
                mixture(m, x_views, a["moe_w12"], a["moe_w3"], weights, acc)
                with m.block() as block:
                    @block.vector
                    def _(dve):
                        for t in range(TT):
                            dve.scalar_tensor_tensor(res[:, t, :], acc[:, t, :], tanh_g[:, 3:4],
                                                     res[:, t, :], ALU.mult, ALU.add)
        with m.block() as block:
            @block.sync
            def _(sp):
                shown = res if stop in (4, 5, 6, 7, 99) else z
                sp.dma_start(out.rearrange("b (t p) d -> p (b t) d", p=P), shown[:, :, :])\
                  .then_inc(m.stored.sem, 16)
                sp.wait_ge(m.stored.sem, m.stored.at(16))


def turn_weight(m, ident, src, row_chunks, col_chunks, dst, col_sizes=None):
    sizes = col_sizes or [P] * col_chunks
    groups = [(c, r) for c in range(col_chunks) for r in range(0, len(row_chunks), 4)]
    with m.block() as block:
        def extent(c, r):
            rows = row_chunks[r:r + 4]
            return sizes[c], r * P, sum(rows)

        @block.tensor
        def _(pe):
            for g, (c, r) in enumerate(groups):
                if g >= 8:
                    pe.wait_ge(m.low_done.sem, m.low_done.at(g - 7))
                for j, rows in enumerate(row_chunks[r:r + 4]):
                    ins = pe.transpose(m.psum[0:sizes[c], g % 8, j * P:j * P + rows],
                                       src[0:rows, r + j, c * P:c * P + sizes[c]], ident[0:rows, 0:rows])
                ins.then_inc(m.products.sem, 1)

        @block.scalar
        def _(act):
            for g, (c, r) in enumerate(groups):
                n, at, size = extent(c, r)
                act.wait_ge(m.products.sem, m.products.at(g + 1))
                act.activation(dst[0][0:n, c, at:at + size], m.psum[0:n, g % 8, 0:size],
                               ACT.Copy).then_inc(m.high_done.sem, 1)

        @block.vector
        def _(dve):
            for g, (c, r) in enumerate(groups):
                n, at, size = extent(c, r)
                dve.wait_ge(m.high_done.sem, m.high_done.at(g + 1))
                dve.tensor_tensor(dst[1][0:n, c, at:at + size], m.psum[0:n, g % 8, 0:size],
                                  dst[0][0:n, c, at:at + size], ALU.subtract).then_inc(m.low_done.sem, 1)

    m.products.close(len(groups))
    m.high_done.close(len(groups))
    m.low_done.close(len(groups))


STOP = 99


def kernel(**inputs):
    import numpy as np
    import concourse.bacc as bacc
    from concourse import mybir as _mybir
    from concourse.bass_utils import run_bass_kernel_spmd

    arrays = {k: np.asarray(v) for k, v in inputs.items()}
    moved = ["ctx_1024", "L1_ffn_Wg", "L1_ffn_W1", "L1_ffn_W2", "L1_ffn_W3", "L1_ffn_Ws1", "L1_ffn_Ws2",
             "L1_ffn_Ws3"]
    laid = {k: v for k, v in arrays.items() if k not in moved}
    laid["ctx_t"] = arrays["ctx_1024"].reshape(-1, 256).T
    for name in ("cq_b", "ck_b", "sq_b", "sk_b", "fi_b"):
        laid[f"L0_xattn_{name}_columns"] = laid.pop("L0_xattn_" + name).reshape(-1, 128).T
    laid["L1_ffn_Wg_t"] = arrays["L1_ffn_Wg"].T
    w1 = np.concatenate([arrays["L1_ffn_Ws1"][None], arrays["L1_ffn_W1"]])
    w2 = np.concatenate([arrays["L1_ffn_Ws2"][None], arrays["L1_ffn_W2"]])
    w3 = np.concatenate([arrays["L1_ffn_Ws3"][None], arrays["L1_ffn_W3"]])
    w12 = np.stack([w1, w2], 1)
    w12 = w12.transpose(0, 3, 1, 2).reshape(9, 2, 128, 2, 682)
    laid["moe_w12"] = w12.transpose(0, 2, 1, 3, 4).reshape(9, 128, 4 * 682)
    laid["moe_w3"] = w3.transpose(0, 2, 1)
    laid["identity"] = np.eye(128, dtype=np.float32)
    nc = bacc.Bacc("TRN2", target_bir_lowering=False, num_devices=1)
    feeds, aps = {}, {}
    for name, v in laid.items():
        v = np.ascontiguousarray(v)
        feeds["in_" + name] = v
        aps[name] = nc.dram_tensor("in_" + name, v.shape, _mybir.dt.from_np(v.dtype),
                                   kind="ExternalInput").ap()
    out = nc.dram_tensor("out_x", (2, 512, 256), _mybir.dt.float32, kind="ExternalOutput").ap()
    flamingo_gated_kernel(nc, aps, out, STOP)
    got = run_bass_kernel_spmd(nc, [feeds], core_ids=[0])
    return got.results[0]["out_x"]
```

```python
from contextlib import ExitStack, contextmanager

import concourse.bass as bass
from concourse import mybir

F32 = mybir.dt.float32
F16 = mybir.dt.float16
BF16 = mybir.dt.bfloat16
U32 = mybir.dt.uint32
ALU = mybir.AluOpType
ACT = mybir.ActivationFunctionType
AX = mybir.AxisListType

P = 128
B, NQ, NCTX, D = 2, 512, 1024, 256
T = B * NQ
TT = T // P
QT = NQ // P
KC = D // P
BANK = 512
EPS = 1e-5
HEAD_W = 16
PAIRS = B * D // HEAD_W
V_COLS = 32
MASK_FLOOR = -60000.0
LN_P_SCALE = 10 * 0.6931471805599453

FP4_BLOCK = 16
SPLIT_TWO_BITS = 4194305.0
HALF_GRID = 6291456.0
TIE_DOWN = 1.0 - 2.0 ** -23


class Signal:

    def __init__(self, sem):
        self.sem = sem
        self.base = 0

    def at(self, n):
        return self.base + n

    def close(self, n):
        self.base += n


class Chain:

    def __init__(self, sem):
        self.sem = sem
        self.count = 0
        self.offset = None

    def step(self, eng, ins):
        ins.then_inc(self.sem, 1)
        self.count += 1
        eng.wait_ge(self.sem, self.count if self.offset is None else self.offset + self.count)

    @contextmanager
    def loop(self, i, steps, trips):
        before = self.count
        self.offset = i * steps
        yield
        assert self.count == before + steps, (self.count - before, steps)
        self.offset = None
        self.count = before + steps * trips


class Machine:

    def __init__(self, nc, ctx):
        self.nc = nc
        self.ctx = ctx

        def signal(name):
            return Signal(ctx.enter_context(nc.semaphore(name)))

        self.loaded = signal("loaded")
        self.stored = signal("stored")
        self.products = signal("products")
        self.high_done = signal("high_done")
        self.low_done = signal("low_done")
        self.evacuated = signal("evacuated")
        self.variance = signal("variance")
        self.deviation = signal("deviation")
        self.ready = signal("ready")
        self.act_ready = signal("act_ready")
        self.operands = (signal("operands_even"), signal("operands_odd"))
        self.maxima = signal("maxima")
        self.stack_loaded = tuple(signal(f"stack_loaded_{i}") for i in range(4))
        self.values_loaded = (signal("values_loaded_even"), signal("values_loaded_odd"))
        self.shift_loaded = (signal("shift_loaded_even"), signal("shift_loaded_odd"))
        self.candidates = signal("candidates")
        self.maxed = signal("maxed")
        self.negated = signal("negated")
        self.row_made = signal("row_made")
        self.row_copied = signal("row_copied")
        self.drawn = signal("drawn")
        self.turned = signal("turned")
        self.probs = signal("probs")
        self.scores = signal("scores")
        self.probs_t = signal("probs_t")
        self.weighted = signal("weighted")
        self.finished = signal("finished")
        self.down_done = signal("down_done")
        self.w12_loaded = signal("w12_loaded")
        self.w3_loaded = signal("w3_loaded")
        self.w12_high = signal("w12_high")
        self.w12_low = signal("w12_low")
        self.w3_high = signal("w3_high")
        self.w3_low = signal("w3_low")
        self.vchain = Chain(ctx.enter_context(nc.semaphore("vchain")))
        self.achain = Chain(ctx.enter_context(nc.semaphore("achain")))
        self.pchain = Chain(ctx.enter_context(nc.semaphore("pchain")))
        ahead = (self.evacuated, self.down_done, self.w12_low, self.w3_low, self.products,
                 self.weighted, self.low_done, self.high_done, self.scores, self.probs, self.finished,
                 self.maxed, self.drawn, self.turned, self.row_copied, self.negated)
        with nc.Block(no_gpsimd_drain=True) as block:
            @block.sync
            def _(sp):
                for s in ahead:
                    sp.sem_inc(s.sem, 1)
        for s in ahead:
            s.close(1)
        self.psum = ctx.enter_context(nc.psum_tensor("psum", [P, 8, BANK], F32))

    def block(self):
        return self.nc.Block(no_gpsimd_drain=True)


def three_terms(pe, out, w_hi, w_lo, x_hi, x_lo, first, last):
    pe.matmul(out, w_hi, x_hi, start=first, stop=False)
    pe.matmul(out, w_hi, x_lo, start=False, stop=False)
    return pe.matmul(out, w_lo, x_hi, start=False, stop=last)


def load_split(m, items):
    with m.block() as block:
        @block.sync
        def _(sp):
            for staging, source, _, _ in items:
                sp.dma_start(staging, source).then_inc(m.loaded.sem, 16)

        @block.scalar
        def _(act):
            act.wait_ge(m.loaded.sem, m.loaded.at(16 * len(items)))
            for staging, _, high, _ in items:
                act.activation(high, staging, ACT.Copy).then_inc(m.high_done.sem, 1)

        @block.vector
        def _(dve):
            for n, (staging, _, high, low) in enumerate(items):
                dve.wait_ge(m.high_done.sem, m.high_done.at(n + 1))
                dve.tensor_tensor(low, staging, high, ALU.subtract)

    m.loaded.close(16 * len(items))
    m.high_done.close(len(items))


def layer_norm(m, tmp, src, dst, gamma=None, beta=None):
    stats, mv, rstd = tmp["stats"], tmp["mv"], tmp["rstd"]
    with m.block() as block:
        @block.vector
        def _(dve):
            for t in range(TT):
                dve.bn_stats(stats[:, t, :], src[:, t, :]).then_inc(m.ready.sem, 1)
            for t in range(TT):
                dve.wait_ge(m.ready.sem, m.ready.at(t + 1))
                dve.bn_aggr(mv[:, t, :], stats[:, t, :]).then_inc(m.ready.sem, 1)
            dve.wait_ge(m.ready.sem, m.ready.at(2 * TT))
            dve.tensor_scalar(rstd[:, :], mv[:, :, 1], EPS, None, ALU.add).then_inc(m.variance.sem, 1)
            dve.wait_ge(m.deviation.sem, m.deviation.at(1))
            m.vchain.step(dve, dve.reciprocal(rstd[:, :], rstd[:, :]))
            for t in range(TT):
                out = dve.tensor_scalar(dst[:, t, :], src[:, t, :], mv[:, t, 0:1], rstd[:, t:t + 1],
                                        ALU.subtract, ALU.mult)
                if gamma is not None:
                    m.vchain.step(dve, out)
                    m.vchain.step(dve, dve.tensor_tensor(dst[:, t, :], dst[:, t, :], gamma, ALU.mult))
                    dve.tensor_tensor(dst[:, t, :], dst[:, t, :], beta, ALU.add)

        @block.scalar
        def _(act):
            act.wait_ge(m.variance.sem, m.variance.at(1))
            act.activation(rstd[:, :], rstd[:, :], ACT.Sqrt).then_inc(m.deviation.sem, 1)

    m.ready.close(2 * TT)
    m.variance.close(1)
    m.deviation.close(1)


def transpose_split(m, ident, source, chunks, high, low):
    banks = (len(chunks) + 3) // 4
    slots = 8 // banks
    with m.block() as block:
        @block.tensor
        def _(pe):
            for t in range(TT):
                if t >= slots:
                    pe.wait_ge(m.low_done.sem, m.low_done.at(t - slots + 1))
                for c, width in enumerate(chunks):
                    bank = (t % slots) * banks + c // 4
                    ins = pe.transpose(m.psum[0:width, bank, (c % 4) * P:(c % 4 + 1) * P],
                                       source(t, c), ident)
                ins.then_inc(m.products.sem, 1)

        def pieces(t):
            full = len([w for w in chunks if w == P])
            spans = [(c, min(c + 4, full), P) for c in range(0, full, 4)]
            spans += [(c, c + 1, chunks[c]) for c in range(full, len(chunks))]
            for a, b, rows in spans:
                bank = (t % slots) * banks + a // 4
                view = m.psum[0:rows, bank, (a % 4) * P:(a % 4 + b - a) * P]
                yield a, b, rows, view.rearrange("p (c q) -> p c q", q=P)

        @block.scalar
        def _(act):
            for t in range(TT):
                act.wait_ge(m.products.sem, m.products.at(t + 1))
                for a, b, rows, view in pieces(t):
                    ins = act.activation(high[0:rows, a:b, t * P:(t + 1) * P], view, ACT.Copy)
                ins.then_inc(m.high_done.sem, 1)

        @block.vector
        def _(dve):
            for t in range(TT):
                dve.wait_ge(m.high_done.sem, m.high_done.at(t + 1))
                for a, b, rows, view in pieces(t):
                    ins = dve.tensor_tensor(low[0:rows, a:b, t * P:(t + 1) * P], view,
                                            high[0:rows, a:b, t * P:(t + 1) * P], ALU.subtract)
                ins.then_inc(m.low_done.sem, 1)

    m.products.close(TT)
    m.high_done.close(TT)
    m.low_done.close(TT)


def project_transposed(m, w, x, out, n_out, n_tok, bias=None):
    groups = [(c, h) for c in range(n_out) for h in range(n_tok // BANK)]
    with m.block() as block:
        @block.tensor
        def _(pe):
            for g, (c, h) in enumerate(groups):
                if g >= 8:
                    pe.wait_ge(m.low_done.sem, m.low_done.at(g - 7))
                for k in range(KC):
                    ins = three_terms(pe, m.psum[:, g % 8, :],
                                      w[0][:, k, c * P:(c + 1) * P], w[1][:, k, c * P:(c + 1) * P],
                                      x[0][:, k, h * BANK:(h + 1) * BANK],
                                      x[1][:, k, h * BANK:(h + 1) * BANK], k == 0, k == KC - 1)
                ins.then_inc(m.products.sem, 1)

        @block.scalar
        def _(act):
            for g, (c, h) in enumerate(groups):
                act.wait_ge(m.products.sem, m.products.at(g + 1))
                dst = out[0][:, c, h * BANK:(h + 1) * BANK]
                if bias is None:
                    ins = act.activation(dst, m.psum[:, g % 8, :], ACT.Copy)
                else:
                    ins = act.activation(dst, m.psum[:, g % 8, :], ACT.Identity, bias=bias[:, c:c + 1])
                ins.then_inc(m.high_done.sem, 1)

        @block.vector
        def _(dve):
            for g, (c, h) in enumerate(groups):
                dve.wait_ge(m.high_done.sem, m.high_done.at(g + 1))
                hi = out[0][:, c, h * BANK:(h + 1) * BANK]
                lo = out[1][:, c, h * BANK:(h + 1) * BANK]
                if bias is None:
                    ins = dve.tensor_tensor(lo, m.psum[:, g % 8, :], hi, ALU.subtract)
                else:
                    ins = dve.scalar_tensor_tensor(lo, m.psum[:, g % 8, :], bias[:, c:c + 1], hi,
                                                   ALU.add, ALU.subtract)
                ins.then_inc(m.low_done.sem, 1)

    m.products.close(len(groups))
    m.high_done.close(len(groups))
    m.low_done.close(len(groups))


def project_values(m, w, x, values, n_tiles, heads, dh, ones_row=None, bias_row=None):
    per_entry = n_tiles // B
    width = heads * dh
    with m.block() as block:
        @block.gpsimd
        def _(pool):
            m.pchain.step(pool, pool.memset(values[:, :, :, :, dh:dh + 1], 1.0))

        @block.tensor
        def _(pe):
            for t in range(n_tiles):
                if t >= 8:
                    pe.wait_ge(m.low_done.sem, m.low_done.at(t - 7))
                out = m.psum[:, t % 8, 0:width]
                for k in range(KC):
                    ins = three_terms(pe, out, x[0][:, k, t * P:(t + 1) * P],
                                      x[1][:, k, t * P:(t + 1) * P], w[0][:, k, :], w[1][:, k, :],
                                      k == 0, k == KC - 1 and bias_row is None)
                if bias_row is not None:
                    ins = pe.matmul(out, ones_row, bias_row, start=False, stop=True)
                ins.then_inc(m.products.sem, 1)

        @block.scalar
        def _(act):
            for t in range(n_tiles):
                act.wait_ge(m.products.sem, m.products.at(t + 1))
                act.activation(values[:, t // per_entry, :, t % per_entry, 0:dh],
                               m.psum[:, t % 8, 0:width].rearrange("p (h d) -> p h d", d=dh),
                               ACT.Copy).then_inc(m.high_done.sem, 1)

        @block.vector
        def _(dve):
            for t in range(n_tiles):
                dve.wait_ge(m.high_done.sem, m.high_done.at(t + 1))
                dve.tensor_tensor(values[:, t // per_entry, :, t % per_entry, dh + 1:2 * dh + 1],
                                  m.psum[:, t % 8, 0:width].rearrange("p (h d) -> p h d", d=dh),
                                  values[:, t // per_entry, :, t % per_entry, 0:dh],
                                  ALU.subtract).then_inc(m.low_done.sem, 1)

    m.products.close(n_tiles)
    m.high_done.close(n_tiles)
    m.low_done.close(n_tiles)


def project_narrow_values(m, w, x, values, n_tiles, ones_row, bias_row):
    per_entry = n_tiles // B
    heads = PAIRS // B
    with m.block() as block:
        @block.gpsimd
        def _(pool):
            m.pchain.step(pool, pool.memset(values[:, :, :, HEAD_W:], 1.0))

        @block.tensor
        def _(pe):
            for t in range(n_tiles):
                if t >= 8:
                    pe.wait_ge(m.evacuated.sem, m.evacuated.at(t - 7))
                out = m.psum[:, t % 8, 0:D]
                for k in range(KC):
                    three_terms(pe, out, x[0][:, k, t * P:(t + 1) * P], x[1][:, k, t * P:(t + 1) * P],
                                w[0][:, k, :], w[1][:, k, :], k == 0, False)
                pe.matmul(out, ones_row, bias_row, start=False, stop=True).then_inc(m.products.sem, 1)

        @block.scalar
        def _(act):
            for t in range(n_tiles):
                act.wait_ge(m.products.sem, m.products.at(t + 1))
                first = (t // per_entry) * heads
                act.activation(values[:, first:first + heads, t % per_entry, 0:HEAD_W],
                               m.psum[:, t % 8, 0:D].rearrange("p (h d) -> p h d", d=HEAD_W),
                               ACT.Copy).then_inc(m.evacuated.sem, 1)

    m.products.close(n_tiles)
    m.evacuated.close(n_tiles)


def project_tokens(m, w, x, rows, n, finish, ones_row=None, bias_row=None):
    with m.block() as block:
        @block.tensor
        def _(pe):
            for t in range(TT):
                out = m.psum[:, t, 0:n]
                for k, r in enumerate(rows):
                    ins = three_terms(pe, out, x[0][0:r, k, t * P:(t + 1) * P],
                                      x[1][0:r, k, t * P:(t + 1) * P], w[0][0:r, k, :], w[1][0:r, k, :],
                                      k == 0, k == len(rows) - 1 and bias_row is None)
                if bias_row is not None:
                    ins = pe.matmul(out, ones_row, bias_row, start=False, stop=True)
                ins.then_inc(m.products.sem, 1)

        @block.vector
        def _(dve):
            for t in range(TT):
                dve.wait_ge(m.products.sem, m.products.at(t + 1))
                finish(dve, t, m.psum[:, t, 0:n])

    m.products.close(TT)


def store_heads(m, parts, order, scratch, n_tok):
    rows = parts[0].shape[1] * P
    with m.block() as block:
        @block.sync
        def _(sp):
            for place, s in enumerate(order):
                for b in range(B):
                    sp.dma_start(
                        scratch[b * rows:(b + 1) * rows, place, :].rearrange("(c p) q -> p c q", p=P),
                        parts[s][:, :, b * n_tok:(b + 1) * n_tok]).then_inc(m.stored.sem, 16)
            sp.wait_ge(m.stored.sem, m.stored.at(16 * B * len(order)))

    m.stored.close(16 * B * len(order))


def narrow_attention(m, ident, fold, q_scr, k_scr, values, result, n_keys, mask_rows=None, mask_bias=None):
    nc = m.nc
    rounds = PAIRS // 2
    tiles = n_keys // P
    halves = n_keys // BANK
    units = rounds * tiles
    scale = float(HEAD_W) ** -0.5
    bufs = 4
    body = bufs * tiles
    lead = tiles + 7
    lag = lead // tiles
    masked = mask_rows is not None
    loads = 3 + 2 * masked
    stack = 3 * HEAD_W
    mask_at = 2 * stack
    shift_at = mask_at + 1
    all_rows = shift_at + 2
    start = 3
    loops = (units - start - lead) // body
    with ExitStack() as mem:
        def sb(name, shape, dt):
            return mem.enter_context(nc.sbuf_tensor(f"{name}_{nc.next_id()}", shape, dt))

        q_buf = sb("q_buf", [P, bufs, NQ], F16)
        k_buf = sb("k_buf", [P, bufs, 2, n_keys], F16)
        ones = sb("ones", [1, n_keys], F16)
        v_buf = sb("v_buf", [P, 2, 2, tiles, V_COLS], F32)
        probs = sb("probs", [P, 4, 2, NQ], F32)
        part_max = sb("part_max", [P, 2, 2, QT, halves], F32)
        neg_max = sb("neg_max", [P, 2, 2, QT], F32)
        shift_row = sb("shift_row", [2 * QT, 2, P], F16)
        out_sb = sb("out_sb", [P, NQ], F32)
        recip = sb("recip", [P, QT, 2], F32)

        def score_banks(u):
            return m.psum[:, 2 * (u % 2):2 * (u % 2) + 2, :]

        def candidate_bank(h):
            return m.psum[:, 4 + h, :]

        turned = m.psum[:, 7, 0:QT * 64]
        row_view = m.psum[0:2 * QT, 7, QT * 64:QT * 64 + P]

        def has(base, u):
            return not isinstance(base, int) or 0 <= base + u < units

        def pe_step(pe, base, base_round, k):
            u = k + 2
            if has(base, u):
                r, j = divmod(u, tiles)
                if j == 0:
                    pe.wait_ge(m.shift_loaded[r % 2].sem,
                               m.shift_loaded[r % 2].at(0) + (base_round // 2 + (r // 2 + 1)) * 32)
                if not isinstance(base, int) or base + u >= 2:
                    pe.wait_ge(m.probs.sem, m.probs.at(base + (u - 1)))
                for h in range(2):
                    ins = pe.matmul(score_banks(u)[:, h, :],
                                    k_buf[0:all_rows, r % bufs, h, j * P:(j + 1) * P],
                                    q_buf[0:all_rows, r % bufs, :], start=True, stop=True)
                ins.then_inc(m.scores.sem, 1)
            v = k + lead
            if has(base, v):
                r, j = divmod(v, tiles)
                t, c = divmod(j, halves)
                if j == 0:
                    signal = m.stack_loaded[r % bufs]
                    pe.wait_ge(signal.sem,
                               signal.at(0) + (base_round // bufs + (r // bufs + 1)) * (16 * loads))
                for h in range(2):
                    if not isinstance(base, int) or base + v >= 1:
                        pe.wait_ge(m.maxed.sem, m.maxed.at(base * 2 + (2 * v + h - 1)))
                    pe.matmul(candidate_bank(h), q_buf[0:shift_at, r % bufs, t * P:(t + 1) * P],
                              k_buf[0:shift_at, r % bufs, h, c * BANK:(c + 1) * BANK],
                              start=True, stop=True)\
                      .then_inc(m.candidates.sem, 1)
            if k % 2 == 1 and has(base, k):
                r, j = divmod(k, tiles)
                if j == 1:
                    pe.wait_ge(m.values_loaded[r % 2].sem,
                               m.values_loaded[r % 2].at(0) + (base_round // 2 + (r // 2 + 1)) * 16)
                    if not isinstance(base, int) or base_round + r >= 1:
                        pe.wait_ge(m.drawn.sem, m.drawn.at(base_round + r))
                pe.wait_ge(m.probs.sem, m.probs.at(base + (k + 1)))
                for odd in range(2):
                    for h in range(2):
                        at = 64 * odd + 32 * h
                        ins = pe.matmul(m.psum[at:at + V_COLS, 6, :], v_buf[:, r % 2, h, j - 1 + odd, :],
                                        probs[:, (k - 1 + odd) % 4, h, :], start=j == 1,
                                        stop=j == tiles - 1)
                ins.then_inc(m.weighted.sem, 2)
            if k % tiles == 1 and has(base, k - tiles):
                r = k // tiles - 1
                pe.wait_ge(m.drawn.sem, m.drawn.at(base_round + (r + 1)))
                rows = base_round + (r + lag + 1)
                if not isinstance(rows, int) or rows <= rounds:
                    pe.wait_ge(m.row_copied.sem, m.row_copied.at(rows))
                else:
                    pe.wait_ge(m.finished.sem, m.finished.at(base_round + r))
                for t in range(QT):
                    ins = pe.matmul(turned[:, t * 64:(t + 1) * 64],
                                    out_sb[:, t * P:(t + 1) * P], fold, start=True, stop=True)
                ins.then_inc(m.turned.sem, 1)
            if v % tiles == 1 and has(base, v - tiles):
                r = v // tiles - 1
                pe.wait_ge(m.negated.sem, m.negated.at(base_round + (r + 1)))
                if not isinstance(base, int) or base_round + r > lag:
                    pe.wait_ge(m.finished.sem, m.finished.at(base_round + (r - lag)))
                elif base_round + r >= 1:
                    pe.wait_ge(m.row_copied.sem, m.row_copied.at(base_round + r))
                pe.matmul(row_view, neg_max[:, r % 2, :, :].rearrange("p h t -> p (h t)"), ident,
                          start=True, stop=True).then_inc(m.row_made.sem, 1)

        def act_step(act, base, base_round, k):
            if k % tiles == 0 and has(base, k - tiles):
                r = k // tiles - 1
                act.wait_ge(m.weighted.sem, m.weighted.at(base + k))
                if not isinstance(base, int) or base_round + r >= 1:
                    act.wait_ge(m.turned.sem, m.turned.at(base_round + r))
                act.activation(out_sb[:, :], m.psum[:, 6, :], ACT.Copy).then_inc(m.drawn.sem, 1)
            u = k + 1
            if has(base, u):
                act.wait_ge(m.scores.sem, m.scores.at(base + (u + 1)))
                if not isinstance(base, int) or base + u >= 4:
                    act.wait_ge(m.weighted.sem, m.weighted.at(base + (u - 3)))
                bias = 0.0
                if masked:
                    bias = mask_bias[:, base + u:base + u + 1] if isinstance(base, int) else \
                        mask_bias[:, bass.ds(base + u, 1)]
                act.activation(probs[:, u % 4, :, :], score_banks(u), ACT.Exp, bias=bias,
                               scale=scale).then_inc(m.probs.sem, 1)
            v = k + lead
            if v % tiles == 1 and has(base, v - tiles):
                r = v // tiles - 1
                act.wait_ge(m.row_made.sem, m.row_made.at(base_round + (r + 1)))
                act.activation(shift_row[:, r % 2, :], row_view, ACT.Copy).then_inc(m.row_copied.sem, 1)

        def dve_step(dve, base, base_round, k):
            v = k + lead
            if has(base, v):
                r, j = divmod(v, tiles)
                t, c = divmod(j, halves)
                for h in range(2):
                    dve.wait_ge(m.candidates.sem, m.candidates.at(base * 2 + (2 * v + h + 1)))
                    if halves > 1:
                        dve.tensor_reduce(part_max[:, r % 2, h, t, c:c + 1], candidate_bank(h), AX.X,
                                          ALU.max).then_inc(m.maxed.sem, 1)
                    else:
                        dve.tensor_reduce(neg_max[:, r % 2, h, t:t + 1], candidate_bank(h), AX.X,
                                          ALU.max, negate=True).then_inc(m.maxed.sem, 1)
                if j == tiles - 1:
                    dve.wait_ge(m.maxed.sem, m.maxed.at(base * 2 + (2 * v + 2)))
                    if halves > 1:
                        dve.tensor_reduce(neg_max[:, r % 2, :, :], part_max[:, r % 2, :, :, :], AX.X,
                                          ALU.max, negate=True).then_inc(m.negated.sem, 1)
                    else:
                        dve.sem_inc(m.negated.sem, 1)
            if k % tiles == 1 and has(base, k - tiles):
                r = k // tiles - 1
                dve.wait_ge(m.turned.sem, m.turned.at(base_round + (r + 1)))
                view = turned.rearrange("p (t h w) -> p t h w", t=QT, h=2)
                m.vchain.step(dve, dve.reciprocal(recip[:, :, :], view[:, :, :, HEAD_W]))
                first = (base_round + r) * 2
                dst = result[:, :, first:first + 2, :] if isinstance(first, int) else \
                    result[:, :, bass.ds(first, 2), :]
                dve.tensor_tensor(dst, view[:, :, :, 0:HEAD_W],
                                  recip[:, :, :].unsqueeze(3).to_broadcast([P, QT, 2, HEAD_W]),
                                  ALU.mult).then_inc(m.finished.sem, 1)

        def rest(eng, step):
            for k in range(start + loops * body, units + 2):
                whole = k // body
                step(eng, whole * body, whole * bufs, k - whole * body)

        with m.block() as block:
            @block.gpsimd
            def _(pool):
                m.pchain.step(pool, pool.memset(ones[:, :], 1.0))
                m.pchain.step(pool, pool.memset(q_buf[mask_at:mask_at + 1, :, :], 1.0))
                m.pchain.step(pool, pool.memset(k_buf[:, :, :, :], 0.0))
                pool.sem_inc(m.ready.sem, 1)

            def load_stack(sp, r, buf):
                sem = m.stack_loaded[buf].sem
                first = r * 2 * HEAD_W
                sp.dma_start(q_buf[0:2 * stack, buf, :],
                             q_scr[bass.ds(first, 2 * HEAD_W), :, :].rearrange("f s q -> (f s) q"))\
                  .then_inc(sem, 16)
                for h in range(2):
                    sp.dma_start(k_buf[h * stack:(h + 1) * stack, buf, h, :],
                                 k_scr[bass.ds(first + h * HEAD_W, HEAD_W), :, :]
                                 .rearrange("f s q -> (f s) q")).then_inc(sem, 16)
                    if masked:
                        sp.dma_start(k_buf[mask_at:mask_at + 1, buf, h, :],
                                     mask_rows[bass.ds(r, 1), :]).then_inc(sem, 16)

            def load_values(sp, r, parity):
                per = 2 * tiles * V_COLS
                sp.dma_start(v_buf[:, parity, :, :, :].rearrange("p h t w -> p (h t w)"),
                             values[:, :, :, :].rearrange("p i t w -> p (i t w)")[:, bass.ds(r * per, per)])\
                  .then_inc(m.values_loaded[parity].sem, 16)

            def load_shift(sp, r, parity, buf):
                sp.wait_ge(m.row_copied.sem, m.row_copied.at(r + 1))
                for h in range(2):
                    row = shift_at + h
                    sp.dma_start(q_buf[row:row + 1, buf, :].rearrange("o (t q) -> o t q", t=QT),
                                 shift_row[h * QT:(h + 1) * QT, parity, :])\
                      .then_inc(m.shift_loaded[parity].sem, 16)

            @block.sync
            def _(sp):
                sp.wait_ge(m.ready.sem, m.ready.at(1))
                for h in range(2):
                    for buf in range(bufs):
                        sp.dma_start(k_buf[shift_at + h:shift_at + h + 1, buf, h, :], ones[:, :])\
                          .then_inc(m.loaded.sem, 16)
                for r in range(bufs):
                    load_stack(sp, r, r)
                for r in range(2):
                    load_values(sp, r, r)
                load_shift(sp, 0, 0, 0)
                with sp.Fori(0, rounds // bufs - 1) as g:
                    for r in range(bufs):
                        load_shift(sp, g * bufs + (r + 1), (r + 1) % 2, (r + 1) % bufs)
                        sp.wait_ge(m.scores.sem, m.scores.at(g * body + (r + 1) * tiles))
                        load_stack(sp, g * bufs + (r + bufs), r)
                        sp.wait_ge(m.weighted.sem, m.weighted.at(g * body + (r + 1) * tiles))
                        load_values(sp, g * bufs + (r + 2), r % 2)
                for r in range(rounds - bufs, rounds - 1):
                    load_shift(sp, r + 1, (r + 1) % 2, (r + 1) % bufs)
                    if r + 2 < rounds:
                        sp.wait_ge(m.weighted.sem, m.weighted.at((r + 1) * tiles))
                        load_values(sp, r + 2, r % 2)

            @block.tensor
            def _(pe):
                pe.wait_ge(m.loaded.sem, m.loaded.at(2 * bufs * 16))
                for k in range(-lead, start):
                    pe_step(pe, 0, 0, k)
                with pe.Fori(0, loops) as g:
                    for k in range(start, start + body):
                        pe_step(pe, g * body, g * bufs, k)
                rest(pe, pe_step)

            @block.scalar
            def _(act):
                for k in range(-lead, start):
                    act_step(act, 0, 0, k)
                with act.Fori(0, loops) as g:
                    for k in range(start, start + body):
                        act_step(act, g * body, g * bufs, k)
                rest(act, act_step)

            @block.vector
            def _(dve):
                for k in range(-lead, start):
                    dve_step(dve, 0, 0, k)
                with dve.Fori(0, loops) as g, m.vchain.loop(g, bufs, loops):
                    for k in range(start, start + body):
                        dve_step(dve, g * body, g * bufs, k)
                rest(dve, dve_step)

    m.ready.close(1)
    m.loaded.close(2 * bufs * 16)
    for signal in m.stack_loaded:
        signal.close(16 * loads * (rounds // bufs))
    for signal in m.shift_loaded:
        signal.close(32 * (rounds // 2))
    for signal in m.values_loaded:
        signal.close(16 * (rounds // 2))
    for signal in (m.scores, m.probs, m.weighted):
        signal.close(units)
    for signal in (m.candidates, m.maxed):
        signal.close(2 * units)
    for signal in (m.negated, m.row_made, m.row_copied, m.drawn, m.turned, m.finished):
        signal.close(rounds)


def wide_attention(m, ident, q_scr, k_scr, values, result, n_keys, heads, dh):
    nc = m.nc
    pairs = B * heads
    units = pairs * QT
    halves = n_keys // BANK
    tiles = n_keys // P
    scale = float(dh) ** -0.5
    out_w = dh + 1
    rows = 2 * dh
    loads = 5
    with ExitStack() as mem:
        def sb(name, shape, dt):
            return mem.enter_context(nc.sbuf_tensor(f"{name}_{nc.next_id()}", shape, dt))

        q_buf = sb("q_buf", [P, 2, NQ], F16)
        k_buf = sb("k_buf", [P, 2, n_keys], F16)
        kl_buf = sb("kl_buf", [P, 2, n_keys], F16)
        probs = sb("probs", [P, 2, n_keys], F32)
        pt_hi = sb("pt_hi", [P, 2, tiles, P], F16)
        pt_lo = sb("pt_lo", [P, 2, tiles, P], F16)
        neg_max = sb("neg_max", [P, 4], F32)
        shift = sb("shift", [P, 4], F32)
        recip = sb("recip", [P, 2, QT], F32)

        def score_bank(u, h):
            return m.psum[:, (u % 2) * 2 + h, :]

        def turn_bank(u, h):
            return m.psum[:, 4 + (u * halves + h) % 2, :]

        def out_bank(head):
            return m.psum[:, 6 + head % 2, 0:QT * out_w].rearrange("p (t w) -> p t w", w=out_w)

        def pe_step(pe, base, k, pair):
            first = isinstance(base, int) and base + k
            if not (isinstance(base, int) and base + k + 3 >= units):
                u = k + 3
                if u % QT == 0:
                    head = u // QT
                    pe.wait_ge(m.operands[head % 2].sem,
                               m.operands[head % 2].at(0) + 16 * loads * (pair(2 * (head // 2)) // 2 + 1)
                               if isinstance(base, int) else
                               m.operands[head % 2].at(0) + loaded_at(base, head))
                if not (isinstance(base, int) and base + u < 2):
                    pe.wait_ge(m.probs.sem, m.probs.at(base + (u - 1)))
                par = (u // QT) % 2
                t = u % QT
                for h in range(halves):
                    out = score_bank(u, h)
                    cols = slice(h * BANK, (h + 1) * BANK)
                    pe.matmul(out, q_buf[0:rows, par, t * P:(t + 1) * P],
                              k_buf[0:rows, par, cols], start=True, stop=False)
                    ins = pe.matmul(out, q_buf[0:dh, par, t * P:(t + 1) * P],
                                    kl_buf[0:dh, par, cols], start=False, stop=True)
                ins.then_inc(m.scores.sem, 1)
            if not (isinstance(base, int) and (base + k + 1 < 0 or base + k + 1 >= units)):
                u = k + 1
                pe.wait_ge(m.probs.sem, m.probs.at(base + (u + 1)))
                for h in range(halves):
                    if not (isinstance(base, int) and (base + u) * halves + h < 2):
                        pe.wait_ge(m.low_done.sem, m.low_done.at(base * halves + (u * halves + h - 1)))
                    for j in range(BANK // P):
                        ins = pe.transpose(turn_bank(u, h)[:, j * P:(j + 1) * P],
                                           probs[:, u % 2, h * BANK + j * P:h * BANK + (j + 1) * P],
                                           ident)
                    ins.then_inc(m.probs_t.sem, 1)
            if not (isinstance(base, int) and base + k < 0):
                u = k
                t = u % QT
                head = u // QT
                if t == 0:
                    pe.wait_ge(m.finished.sem, m.finished.at(pair(head)))
                pe.wait_ge(m.low_done.sem, m.low_done.at(base * halves + (u + 1) * halves))
                out = out_bank(head)[:, t, :]
                for j in range(tiles):
                    hi, lo = pt_hi[:, u % 2, j, :], pt_lo[:, u % 2, j, :]
                    v = values_of(pair(head), j)
                    pe.matmul(out, hi, v(0, dh + 1), start=j == 0, stop=False)
                    pe.matmul(out[:, 0:dh], hi, v(dh + 1, 2 * dh + 1), start=False, stop=False)
                    ins = pe.matmul(out, lo, v(0, dh + 1), start=False, stop=j == tiles - 1)
                ins.then_inc(m.weighted.sem, 1)

        vw = 2 * dh + 1
        flat = values[:, :, :, :, :].rearrange("p b h t w -> p (b h t w)")

        def values_of(i, j):
            def cols(a, b):
                at = i * (tiles * vw) + (j * vw + a)
                return flat[:, bass.ds(at, b - a)] if not isinstance(at, int) else flat[:, at:at + b - a]
            return cols

        def loaded_at(base, head):
            return (base // 8 + (head // 2 + 1)) * (16 * loads)

        def act_step(act, base, k):
            if not (isinstance(base, int) and (base + k + 2 < 0 or base + k + 2 >= units)):
                u = k + 2
                act.wait_ge(m.maxima.sem, m.maxima.at(base + (u + 1)))
                if not (isinstance(base, int) and base + u < 2):
                    act.wait_ge(m.probs_t.sem, m.probs_t.at(base * halves + (u - 1) * halves))
                act.activation(probs[:, u % 2, :], m.psum[:, (u % 2) * 2:(u % 2) * 2 + halves, :]
                               .rearrange("p h q -> p (h q)"), ACT.Exp, bias=shift[:, u % 4:u % 4 + 1],
                               scale=scale).then_inc(m.probs.sem, 1)
            if not (isinstance(base, int) and (base + k + 1 < 0 or base + k + 1 >= units)):
                u = k + 1
                for h in range(halves):
                    act.wait_ge(m.probs_t.sem, m.probs_t.at(base * halves + (u * halves + h + 1)))
                    if h == 0 and not (isinstance(base, int) and base + u < 2):
                        act.wait_ge(m.weighted.sem, m.weighted.at(base + (u - 1)))
                    act.activation(pt_hi[:, u % 2, h * 4:(h + 1) * 4, :],
                                   turn_bank(u, h).rearrange("p (j q) -> p j q", q=P),
                                   ACT.Copy).then_inc(m.high_done.sem, 1)

        def dve_step(dve, base, k, pair):
            if not (isinstance(base, int) and base + k < 0):
                u = k
                for h in range(halves):
                    dve.wait_ge(m.high_done.sem, m.high_done.at(base * halves + (u * halves + h + 1)))
                    dve.tensor_tensor(pt_lo[:, u % 2, h * 4:(h + 1) * 4, :],
                                      turn_bank(u, h).rearrange("p (j q) -> p j q", q=P),
                                      pt_hi[:, u % 2, h * 4:(h + 1) * 4, :],
                                      ALU.subtract).then_inc(m.low_done.sem, 1)
            if not (isinstance(base, int) and base + k + 3 >= units):
                u = k + 3
                dve.wait_ge(m.scores.sem, m.scores.at(base + (u + 1)))
                m.vchain.step(dve, dve.tensor_reduce(
                    neg_max[:, u % 4:u % 4 + 1], m.psum[:, (u % 2) * 2:(u % 2) * 2 + halves, :],
                    AX.XY, ALU.max, negate=True))
                dve.tensor_scalar(shift[:, u % 4:u % 4 + 1], neg_max[:, u % 4:u % 4 + 1], scale,
                                  LN_P_SCALE, ALU.mult, ALU.add).then_inc(m.maxima.sem, 1)
            if k % QT == 1 and not (isinstance(base, int) and base + k < QT):
                normalise(dve, base, k // QT - 1, pair)

        def normalise(dve, base, head, pair):
            dve.wait_ge(m.weighted.sem, m.weighted.at(base + (head + 1) * QT))
            out = out_bank(head)
            r = recip[:, head % 2, :]
            m.vchain.step(dve, dve.reciprocal(r, out[:, :, dh]))
            rb = r.unsqueeze(2).to_broadcast([P, QT, dh])
            i = pair(head)
            dst = result[:, :, i, :] if isinstance(i, int) else \
                result[:, :, bass.ds(i, 1), :].rearrange("p t o d -> p t (o d)")
            dve.tensor_tensor(dst, out[:, :, 0:dh], rb, ALU.mult).then_inc(m.finished.sem, 1)

        rounds = units // 8

        with m.block() as block:
            def load(sp, i, par):
                sem = m.operands[par].sem
                head = bass.ds(i * dh, dh)
                for s, at in ((0, 0), (1, 1)):
                    sp.dma_start(q_buf[at * dh:(at + 1) * dh, par, :], q_scr[head, s, :]).then_inc(sem, 16)
                for at in range(2):
                    sp.dma_start(k_buf[at * dh:(at + 1) * dh, par, :], k_scr[head, 0, :]).then_inc(sem, 16)
                sp.dma_start(kl_buf[0:dh, par, :], k_scr[head, 1, :]).then_inc(sem, 16)

            @block.sync
            def _(sp):
                load(sp, 0, 0)
                load(sp, 1, 1)
                with sp.Fori(0, pairs // 2 - 1) as j:
                    for par in range(2):
                        sp.wait_ge(m.scores.sem, m.scores.at(j * 8 + 4 * (par + 1)))
                        load(sp, j * 2 + (2 + par), par)

            @block.tensor
            def _(pe):
                def static_pair(base):
                    return lambda head: base // QT + head
                for k in range(-3, 0):
                    pe_step(pe, 0, k, static_pair(0))
                with pe.Fori(0, rounds - 1) as j:
                    for k in range(8):
                        pe_step(pe, j * 8, k, lambda head: j * 2 + head)
                for k in range(8):
                    pe_step(pe, 8 * (rounds - 1), k, static_pair(8 * (rounds - 1)))

            @block.scalar
            def _(act):
                for k in range(-3, 0):
                    act_step(act, 0, k)
                with act.Fori(0, rounds - 1) as j:
                    for k in range(8):
                        act_step(act, j * 8, k)
                for k in range(8):
                    act_step(act, 8 * (rounds - 1), k)

            @block.vector
            def _(dve):
                dve.sem_inc(m.finished.sem, 1)
                for k in range(-3, 0):
                    dve_step(dve, 0, k, lambda head: head)
                for k in range(8):
                    dve_step(dve, 0, k, lambda head: head)
                with dve.Fori(0, rounds - 2) as r, m.vchain.loop(r, 10, rounds - 2):
                    for k in range(8):
                        dve_step(dve, r * 8 + 8, k, lambda head: r * 2 + (head + 2))
                last = 8 * (rounds - 1)
                for k in range(8):
                    dve_step(dve, last, k, lambda head: last // QT + head)
                normalise(dve, last, 1, lambda head: last // QT + head)

    for par in range(2):
        m.operands[par].close(16 * loads * (pairs // 2))
    m.scores.close(units)
    m.maxima.close(units)
    m.probs.close(units)
    m.probs_t.close(units * halves)
    m.high_done.close(units * halves)
    m.low_done.close(units * halves)
    m.weighted.close(units)
    m.finished.close(pairs + 1)


def quantise(m, tmp, src, dst, n_blocks):
    rows = src.shape[0]
    size = n_blocks * FP4_BLOCK
    amax, inv = tmp["amax"][0:rows, 0:n_blocks], tmp["inv"][0:rows, 0:n_blocks]
    xn, mag, spl, fine = (tmp["quant"][0:rows, j, 0:size] for j in range(4))

    def blocks(a):
        return a.rearrange("p (n b) -> p n b", b=FP4_BLOCK)

    def program(dve):
        step = m.vchain.step
        step(dve, dve.tensor_reduce(amax, src, AX.X, ALU.max, apply_absolute_value=True))
        step(dve, dve.tensor_scalar(amax, amax, 1.0 / 6.0, 1e-12, ALU.mult, ALU.max))
        step(dve, dve.reciprocal(inv, amax))
        step(dve, dve.tensor_scalar(inv, inv, TIE_DOWN, None, ALU.mult))
        step(dve, dve.tensor_tensor(blocks(xn), src, inv.unsqueeze(2).to_broadcast([rows, n_blocks, FP4_BLOCK]),
                                    ALU.mult))
        step(dve, dve.tensor_scalar(mag.bitcast(U32), xn.bitcast(U32), 0x7FFFFFFF, None,
                                    ALU.bitwise_and))
        step(dve, dve.tensor_scalar(fine, mag, 1.0, HALF_GRID, ALU.min, ALU.add))
        step(dve, dve.tensor_scalar(mag, mag, 1.0, None, ALU.max))
        step(dve, dve.scalar_tensor_tensor(spl, mag, SPLIT_TWO_BITS, mag, ALU.mult, ALU.subtract))
        step(dve, dve.scalar_tensor_tensor(spl, mag, SPLIT_TWO_BITS, spl, ALU.mult, ALU.subtract))
        step(dve, dve.scalar_tensor_tensor(mag, fine, HALF_GRID + 1.0, spl, ALU.subtract, ALU.add))
        step(dve, dve.tensor_scalar(xn.bitcast(U32), xn.bitcast(U32), 0x80000000, None, ALU.bitwise_and))
        step(dve, dve.tensor_tensor(mag.bitcast(U32), mag.bitcast(U32), xn.bitcast(U32), ALU.bitwise_or))
        step(dve, dve.tensor_tensor(dst, blocks(mag),
                                    amax.unsqueeze(2).to_broadcast([rows, n_blocks, FP4_BLOCK]), ALU.mult))
    return program


def feed_forward_gelu(m, w, x, out, bias, n_out):
    groups = [(c, h) for c in range(n_out) for h in range(T // BANK)]
    nc = m.nc
    with nc.sbuf_tensor("gelu_out", [P, 2, BANK], F32) as full, m.block() as block:
        @block.tensor
        def _(pe):
            for g, (c, h) in enumerate(groups):
                if g >= 8:
                    pe.wait_ge(m.act_ready.sem, m.act_ready.at(g - 7))
                for k in range(KC):
                    ins = three_terms(pe, m.psum[:, g % 8, :],
                                      w[0][:, k, c * P:(c + 1) * P], w[1][:, k, c * P:(c + 1) * P],
                                      x[0][:, k, h * BANK:(h + 1) * BANK],
                                      x[1][:, k, h * BANK:(h + 1) * BANK], k == 0, k == KC - 1)
                ins.then_inc(m.products.sem, 1)

        @block.scalar
        def _(act):
            for g, (c, h) in enumerate(groups):
                act.wait_ge(m.products.sem, m.products.at(g + 1))
                if g >= 2:
                    act.wait_ge(m.low_done.sem, m.low_done.at(g - 1))
                act.activation(full[:, g % 2, :], m.psum[:, g % 8, :], ACT.Gelu,
                               bias=bias[:, c:c + 1]).then_inc(m.act_ready.sem, 1)

        @block.vector
        def _(dve):
            for g, (c, h) in enumerate(groups):
                hi = out[0][:, c, h * BANK:(h + 1) * BANK]
                dve.wait_ge(m.act_ready.sem, m.act_ready.at(g + 1))
                m.vchain.step(dve, dve.tensor_copy(hi, full[:, g % 2, :]))
                dve.tensor_tensor(out[1][:, c, h * BANK:(h + 1) * BANK], full[:, g % 2, :], hi,
                                  ALU.subtract).then_inc(m.low_done.sem, 1)

    m.products.close(len(groups))
    m.act_ready.close(len(groups))
    m.low_done.close(len(groups))


FFN_H = 704
FFN_BLOCKS = FFN_H // FP4_BLOCK
FFN_ROWS = [P] * (FFN_H // P) + [FFN_H % P]
MOE_H = 682
MOE_ROWS = [P] * (MOE_H // P) + [MOE_H % P]
MOE_CH = len(MOE_ROWS)
EXPERTS, TOP = 8, 4
SLOTS = EXPERTS + 1


def gate_up(m, x, wg, wu, hid):
    half = FFN_H // 2
    with m.nc.sbuf_tensor("silu_out", [P, 2, 2, half], F32) as silu, m.block() as block:
        @block.tensor
        def _(pe):
            for t in range(TT):
                if t >= 2:
                    pe.wait_ge(m.low_done.sem, m.low_done.at(t - 1))
                for a, w in enumerate((wg, wu)):
                    for s in range(2):
                        out = m.psum[:, (t % 2) * 4 + 2 * a + s, 0:half]
                        for k in range(KC):
                            ins = three_terms(pe, out, x[0][:, k, t * P:(t + 1) * P],
                                              x[1][:, k, t * P:(t + 1) * P],
                                              w[0][:, k, s * half:(s + 1) * half],
                                              w[1][:, k, s * half:(s + 1) * half], k == 0, k == KC - 1)
                    ins.then_inc(m.products.sem, 1)

        @block.scalar
        def _(act):
            for t in range(TT):
                act.wait_ge(m.products.sem, m.products.at(2 * t + 1))
                if t >= 2:
                    act.wait_ge(m.low_done.sem, m.low_done.at(t - 1))
                act.activation(silu[:, t % 2, :, :], m.psum[:, (t % 2) * 4:(t % 2) * 4 + 2, 0:half],
                               ACT.Silu).then_inc(m.act_ready.sem, 1)

        @block.vector
        def _(dve):
            for t in range(TT):
                dve.wait_ge(m.act_ready.sem, m.act_ready.at(t + 1))
                dve.wait_ge(m.products.sem, m.products.at(2 * t + 2))
                dve.tensor_tensor(hid[:, t, :].rearrange("p (s q) -> p s q", s=2),
                                  m.psum[:, (t % 2) * 4 + 2:(t % 2) * 4 + 4, 0:half],
                                  silu[:, t % 2, :, :], ALU.mult).then_inc(m.low_done.sem, 1)

    m.products.close(2 * TT)
    m.act_ready.close(TT)
    m.low_done.close(TT)


def route(m, tmp, gate, weights):
    nc = m.nc
    with ExitStack() as mem:
        beats = mem.enter_context(nc.sbuf_tensor("beats", [P, TT, EXPERTS, EXPERTS], F32))
        rank = mem.enter_context(nc.sbuf_tensor("rank", [P, TT, EXPERTS], F32))
        top = mem.enter_context(nc.sbuf_tensor("top", [P, TT], F32))
        with m.block() as block:
            @block.vector
            def _(dve):
                step = m.vchain.step
                step(dve, dve.memset(weights[:, 0, :], 1.0))
                for e in range(EXPERTS):
                    mine = gate[:, :, e:e + 1].to_broadcast([P, TT, EXPERTS])
                    if e:
                        step(dve, dve.tensor_tensor(beats[:, :, e, 0:e], gate[:, :, 0:e], mine[:, :, 0:e],
                                                    ALU.is_ge))
                    step(dve, dve.tensor_tensor(beats[:, :, e, e:EXPERTS], gate[:, :, e:EXPERTS],
                                                mine[:, :, e:EXPERTS], ALU.is_gt))
                step(dve, dve.tensor_reduce(rank[:, :, :], beats[:, :, :, :], AX.X, ALU.add))
                step(dve, dve.tensor_scalar(rank[:, :, :], rank[:, :, :], float(TOP), None, ALU.is_lt))
                step(dve, dve.tensor_reduce(top[:, :], gate[:, :, :], AX.X, ALU.max))
                step(dve, dve.tensor_tensor(gate[:, :, :], gate[:, :, :],
                                            top[:, :].unsqueeze(2).to_broadcast([P, TT, EXPERTS]),
                                            ALU.subtract))
                dve.nop().then_inc(m.ready.sem, 1)
                dve.wait_ge(m.act_ready.sem, m.act_ready.at(1))
                step(dve, dve.tensor_tensor(gate[:, :, :], gate[:, :, :], rank[:, :, :], ALU.mult))
                step(dve, dve.tensor_reduce(top[:, :], gate[:, :, :], AX.X, ALU.add))
                step(dve, dve.reciprocal(top[:, :], top[:, :]))
                step(dve, dve.tensor_tensor(weights[:, 1:SLOTS, :].rearrange("p e t -> p t e"),
                                            gate[:, :, :],
                                            top[:, :].unsqueeze(2).to_broadcast([P, TT, EXPERTS]),
                                            ALU.mult))

            @block.scalar
            def _(act):
                act.wait_ge(m.ready.sem, m.ready.at(1))
                act.activation(gate[:, :, :], gate[:, :, :], ACT.Exp).then_inc(m.act_ready.sem, 1)

    m.ready.close(1)
    m.act_ready.close(1)


def mixture(m, x, w12_dram, w3_dram, weights, acc):
    nc = m.nc
    per = MOE_CH * 2
    with ExitStack() as mem:
        def sb(name, shape, dt):
            return mem.enter_context(nc.sbuf_tensor(name, shape, dt))

        w12 = sb("w12", [P, KC * 2 * MOE_H], F32)
        w3 = sb("w3", [P, MOE_CH, D], F32)
        w12_hi = sb("w12_hi", [P, KC, 2, MOE_H], F16)
        w12_lo = sb("w12_lo", [P, KC, 2, MOE_H], F16)
        w3_hi = sb("w3_hi", [P, MOE_CH, D], F16)
        w3_lo = sb("w3_lo", [P, MOE_CH, D], F16)
        silu = sb("silu", [P, 2, BANK], F32)
        prod = sb("prod", [P, 2, BANK], F32)
        g_hi = sb("g_hi", [P, MOE_CH, T], F16)
        g_lo = sb("g_lo", [P, MOE_CH, T], F16)
        last = SLOTS - 1
        full = MOE_H // P
        tail = MOE_ROWS[-1]

        def up_banks(u):
            return m.psum[:, 2 * (u % 2), :], m.psum[:, 2 * (u % 2) + 1, :]

        def split_w12_high(act, e):
            act.wait_ge(m.w12_loaded.sem, m.w12_loaded.at(e * 16 + 16))
            act.wait_ge(m.products.sem, m.products.at(e * (2 * per)))
            act.activation(w12_hi[:, :, :, :].rearrange("p k w n -> p (k w n)"), w12[:, :],
                           ACT.Copy).then_inc(m.w12_high.sem, 1)

        def split_w12_low(dve, e):
            dve.wait_ge(m.w12_high.sem, m.w12_high.at(e + 1))
            dve.tensor_tensor(w12_lo[:, :, :, :].rearrange("p k w n -> p (k w n)"), w12[:, :],
                              w12_hi[:, :, :, :].rearrange("p k w n -> p (k w n)"),
                              ALU.subtract).then_inc(m.w12_low.sem, 1)

        with m.block() as block:
            @block.sync
            def _(sp):
                with sp.Fori(0, SLOTS) as e:
                    sp.wait_ge(m.w12_low.sem, m.w12_low.at(e))
                    sp.dma_start(w12[:, :], w12_dram[bass.ds(e, 1), :, :].rearrange("o p n -> (o p) n"))\
                      .then_inc(m.w12_loaded.sem, 16)
                    sp.wait_ge(m.w3_low.sem, m.w3_low.at(e))
                    rows = w3_dram[bass.ds(e, 1), :, :].rearrange("o h d -> (o h) d")
                    sp.dma_start(w3[:, 0:full, :], rows[0:full * P, :].rearrange("(c p) d -> p c d", p=P))\
                      .then_inc(m.w3_loaded.sem, 16)
                    sp.dma_start(w3[0:tail, full, :], rows[full * P:MOE_H, :])\
                      .then_inc(m.w3_loaded.sem, 16)

            @block.tensor
            def _(pe):
                with pe.Fori(0, SLOTS) as e:
                    pe.wait_ge(m.w12_low.sem, m.w12_low.at(e + 1))
                    for u in range(per):
                        half, c = divmod(u, MOE_CH)
                        r = MOE_ROWS[c]
                        if u >= 2:
                            pe.wait_ge(m.evacuated.sem, m.evacuated.at(e * per + (u - 1)))
                        else:
                            pe.wait_ge(m.evacuated.sem, m.evacuated.at(e * per))
                        for a in range(2):
                            out = up_banks(u)[a][0:r, :]
                            for k in range(KC):
                                ins = three_terms(pe, out, w12_hi[:, k, a, c * P:c * P + r],
                                                  w12_lo[:, k, a, c * P:c * P + r],
                                                  x[0][:, k, half * BANK:(half + 1) * BANK],
                                                  x[1][:, k, half * BANK:(half + 1) * BANK],
                                                  k == 0, k == KC - 1)
                            ins.then_inc(m.products.sem, 1)
                    pe.wait_ge(m.w3_low.sem, m.w3_low.at(e + 1))
                    for t in range(TT):
                        if t % (TT // 2) == 0:
                            pe.wait_ge(m.low_done.sem, m.low_done.at(e * per + (t // (TT // 2) + 1) * MOE_CH))
                        if t >= 4:
                            pe.wait_ge(m.down_done.sem, m.down_done.at(e * TT + (t - 3)))
                        else:
                            pe.wait_ge(m.down_done.sem, m.down_done.at(e * TT))
                        out = m.psum[:, 4 + t % 4, 0:D]
                        for c, r in enumerate(MOE_ROWS):
                            ins = three_terms(pe, out, g_hi[0:r, c, t * P:(t + 1) * P],
                                              g_lo[0:r, c, t * P:(t + 1) * P],
                                              w3_hi[0:r, c, :], w3_lo[0:r, c, :], c == 0, c == MOE_CH - 1)
                        ins.then_inc(m.weighted.sem, 1)

            def act_expert(act, e, more):
                for u in range(per):
                    half, c = divmod(u, MOE_CH)
                    r = MOE_ROWS[c]
                    act.wait_ge(m.products.sem, m.products.at(e * (2 * per) + (2 * u + 1)))
                    act.wait_ge(m.evacuated.sem, m.evacuated.at(e * per + max(u - 1, 0)))
                    act.activation(silu[0:r, u % 2, :], up_banks(u)[0][0:r, :], ACT.Silu)\
                       .then_inc(m.act_ready.sem, 1)
                    act.wait_ge(m.evacuated.sem, m.evacuated.at(e * per + (u + 1)))
                    act.wait_ge(m.weighted.sem, m.weighted.at(e * TT))
                    act.activation(g_hi[0:r, c, half * BANK:(half + 1) * BANK], prod[0:r, u % 2, :],
                                   ACT.Copy).then_inc(m.high_done.sem, 1)
                    if u == 2:
                        act.wait_ge(m.w3_loaded.sem, m.w3_loaded.at(e * 32 + 32))
                        act.activation(w3_hi[:, 0:full, :], w3[:, 0:full, :], ACT.Copy)\
                           .then_inc(m.w3_high.sem, 1)
                        act.activation(w3_hi[0:tail, full, :], w3[0:tail, full, :], ACT.Copy)\
                           .then_inc(m.w3_high.sem, 1)
                if more:
                    split_w12_high(act, e + 1)

            @block.scalar
            def _(act):
                split_w12_high(act, 0)
                with act.Fori(0, last) as e:
                    act_expert(act, e, True)
                act_expert(act, last, False)

            def dve_expert(dve, e, more):
                for u in range(per):
                    half, c = divmod(u, MOE_CH)
                    r = MOE_ROWS[c]
                    dve.wait_ge(m.act_ready.sem, m.act_ready.at(e * per + (u + 1)))
                    dve.wait_ge(m.products.sem, m.products.at(e * (2 * per) + (2 * u + 2)))
                    dve.wait_ge(m.high_done.sem, m.high_done.at(e * per + max(u - 1, 0)))
                    dve.tensor_tensor(prod[0:r, u % 2, :], up_banks(u)[1][0:r, :], silu[0:r, u % 2, :],
                                      ALU.mult).then_inc(m.evacuated.sem, 1)
                    dve.wait_ge(m.high_done.sem, m.high_done.at(e * per + (u + 1)))
                    dve.tensor_tensor(g_lo[0:r, c, half * BANK:(half + 1) * BANK], prod[0:r, u % 2, :],
                                      g_hi[0:r, c, half * BANK:(half + 1) * BANK],
                                      ALU.subtract).then_inc(m.low_done.sem, 1)
                    if u == 2:
                        dve.wait_ge(m.w3_high.sem, m.w3_high.at(e * 2 + 2))
                        m.vchain.step(dve, dve.tensor_tensor(w3_lo[0:tail, full, :], w3[0:tail, full, :],
                                                             w3_hi[0:tail, full, :], ALU.subtract))
                        dve.tensor_tensor(w3_lo[:, 0:full, :], w3[:, 0:full, :], w3_hi[:, 0:full, :],
                                          ALU.subtract).then_inc(m.w3_low.sem, 1)
                if more:
                    split_w12_low(dve, e + 1)
                for t in range(TT):
                    dve.wait_ge(m.weighted.sem, m.weighted.at(e * TT + (t + 1)))
                    w = weights[:, e, t:t + 1] if isinstance(e, int) else \
                        weights[:, bass.ds(e, 1), t:t + 1].rearrange("p o t -> p (o t)")
                    dve.wait_ge(m.down_done.sem, m.down_done.at(e * TT + 0))
                    dve.scalar_tensor_tensor(acc[:, t, :], m.psum[:, 4 + t % 4, 0:D], w, acc[:, t, :],
                                             ALU.mult, ALU.add).then_inc(m.down_done.sem, 1)

            @block.vector
            def _(dve):
                m.vchain.step(dve, dve.memset(acc[:, :, :], 0.0))
                split_w12_low(dve, 0)
                with dve.Fori(0, last) as e, m.vchain.loop(e, 1, last):
                    dve_expert(dve, e, True)
                dve_expert(dve, last, False)

    m.w12_loaded.close(16 * SLOTS)
    m.w3_loaded.close(32 * SLOTS)
    m.w12_high.close(SLOTS)
    m.w12_low.close(SLOTS)
    m.w3_high.close(2 * SLOTS)
    m.w3_low.close(SLOTS)
    m.products.close(2 * per * SLOTS)
    m.act_ready.close(per * SLOTS)
    m.evacuated.close(per * SLOTS)
    m.high_done.close(per * SLOTS)
    m.low_done.close(per * SLOTS)
    m.weighted.close(TT * SLOTS)
    m.down_done.close(TT * SLOTS)


def flamingo_gated_kernel(nc, a, out, stop=99):
    ctx = ExitStack()
    with ctx:
        m = Machine(nc, ctx)

        used = {}

        def sb(name, shape, dt, scope=ctx):
            used[name] = used.get(name, 0) + 1
            return scope.enter_context(nc.sbuf_tensor(f"{name}_{used[name]}", shape, dt))

        ident = sb("ident", [P, P], F32)
        res = sb("res", [P, TT, D], F32)
        z = sb("z", [P, TT, D], F32)
        x_t = (sb("xt_hi", [P, KC, T], F16), sb("xt_lo", [P, KC, T], F16))
        tanh_g = sb("tanh_g", [P, 4], F32)
        ones_row = sb("ones_row", [1, P], F32)
        fold = sb("fold", [P, 64], F32)
        tmp = {"stats": sb("stats", [P, TT, 6], F32), "mv": sb("mv", [P, TT, 2], F32),
               "rstd": sb("rstd", [P, TT], F32)}
        dram = lambda name, shape, dt: nc.dram_tensor(name, shape, dt, kind="Internal").ap()
        q0_scr = dram("q0_scr", (B * D, 3, NQ), F16)
        k0_scr = dram("k0_scr", (B * D, 3, NCTX), F16)
        k1_scr = dram("k1_scr", (B * D, 3, NQ), F16)
        D1 = 512
        q2_scr = dram("q2_scr", (B * D1, 2, NQ), F16)
        k2_scr = dram("k2_scr", (B * D1, 2, NCTX), F16)
        mask_scr = dram("mask_scr", (PAIRS // 2, NCTX), F16)

        def gated(i):
            def finish(dve, t, view):
                dve.scalar_tensor_tensor(res[:, t, :], view, tanh_g[:, i:i + 1], res[:, t, :],
                                         ALU.mult, ALU.add)
            return finish

        def add_residual(dve, t, view):
            dve.tensor_tensor(z[:, t, :], view, z[:, t, :], ALU.add)

        def load_all(items, extra=None):
            with m.block() as block:
                @block.sync
                def _(sp):
                    for dst, src in items:
                        sp.dma_start(dst, src).then_inc(m.loaded.sem, 16)
                    sp.wait_ge(m.loaded.sem, m.loaded.at(16 * len(items)))
            m.loaded.close(16 * len(items))

        def row(name):
            return a[name].rearrange("(o n) -> o n", o=1)

        def everywhere(name):
            return a[name].rearrange("(o n) -> o n", o=1).partition_broadcast(P) \
                if False else a[name].rearrange("(o n) -> o n", o=1).to_broadcast([P, a[name].shape[0]])

        def weight(name):
            return a[name].rearrange("(c p) n -> p c n", p=P)

        def column(name):
            return a[name + "_columns"]

        load_all([(ident[:, :], a["identity"]), (res[:, :, :], a["x"].rearrange("b (t p) d -> p (b t) d", p=P)),
                  (tanh_g[:, 0:2], everywhere("g_xattn")), (tanh_g[:, 2:4], everywhere("g_ffn"))])
        with m.block() as block:
            @block.scalar
            def _(act):
                act.activation(tanh_g[:, :], tanh_g[:, :], ACT.Tanh)

            @block.gpsimd
            def _(pool):
                m.pchain.step(pool, pool.memset(ones_row[:, :], 1.0))
                m.pchain.step(pool, pool.tensor_tensor(fold[:, :], ident[:, 0:64], ident[:, 64:P], ALU.add))

        def token_source(t, c):
            return z[:, t, c * P:(c + 1) * P]

        def to_x_t():
            transpose_split(m, ident[:, :], token_source, [P] * KC, *(v[:, :, :] for v in x_t))

        x_views = tuple(v[:, :, :] for v in x_t)

        def pair_of(name, shape, scope):
            return tuple(sb(f"{name}_{s}", shape, F16, scope)[tuple([slice(None)] * len(shape))]
                         for s in ("hi", "lo"))

        def split_weights(names, kc, scope):
            outs = [pair_of(name, [P, kc, a[name].shape[1]], scope) for name in names]
            with ExitStack() as staging:
                items = []
                for name, (high, low) in zip(names, outs):
                    st = sb(f"{name}_f32", [P, kc, a[name].shape[1]], F32, staging)
                    items.append((st[:, :, :], weight(name), high, low))
                load_split(m, items)
            return outs

        layer_norm(m, tmp, res, z)
        to_x_t()
        with ExitStack() as s_ctx:
            result = sb("heads_out", [P, QT, B * 16, 16], F32, s_ctx)
            values = sb("values0", [P, PAIRS, NCTX // P, V_COLS], F32, s_ctx)
            mask_bias = sb("mask_bias", [P, B, PAIRS // 2 // B, NCTX // P], F32, s_ctx)
            with ExitStack() as scope:
                wq, wk, wv = split_weights(["L0_xattn_cq_w", "L0_xattn_ck_w", "L0_xattn_cv_w"], KC, scope)
                c_t = split_weights(["ctx_t"], KC, scope)[0]
                qb = sb("qb", [P, KC], F32, scope)
                kb = sb("kb", [P, KC], F32, scope)
                vb = sb("vb", [1, D], F32, scope)
                mask = sb("mask", [P, B, NCTX], F32, scope)
                top = sb("mask_top", [P, B], F32, scope)
                mask_row = sb("mask_row", [1, B, NCTX], F16, scope)
                cols = sb("mask_columns", [P, B, NCTX // P], F32, scope)
                coarse = sb("mask_coarse", [P, B, NCTX // P], F32, scope)
                coarse_16 = sb("mask_coarse_16", [P, B, NCTX // P], F16, scope)
                load_all([(qb[:, :], column("L0_xattn_cq_b")), (kb[:, :], column("L0_xattn_ck_b")),
                          (vb[:, :], row("L0_xattn_cv_b")),
                          (mask[:, :, :].rearrange("p b k -> p (b k)"),
                           a["mask_Bx1x1xS2_ff0"].rearrange("b u v k -> (u v) (b k)")
                           .to_broadcast([P, B * NCTX])),
                          (cols[:, :, :].rearrange("p b t -> p (b t)"), a["mask_columns"])])
                with m.block() as block:
                    @block.vector
                    def _(dve):
                        step = m.vchain.step
                        rounds = PAIRS // 2 // B
                        step(dve, dve.tensor_reduce(top[:, :], mask[:, :, :], AX.X, ALU.max))
                        for b in range(B):
                            step(dve, dve.tensor_scalar(mask[0:1, b, :], mask[0:1, b, :], top[0:1, b:b + 1],
                                                        4.0, ALU.subtract, ALU.mult))
                            step(dve, dve.tensor_scalar(cols[:, b, :], cols[:, b, :], top[:, b:b + 1],
                                                        None, ALU.subtract))
                        step(dve, dve.tensor_scalar(mask_row[:, :, :], mask[0:1, :, :], MASK_FLOOR, None,
                                                    ALU.max))
                        step(dve, dve.tensor_scalar(coarse_16[:, :, :], cols[:, :, :], 4.0, MASK_FLOOR,
                                                    ALU.mult, ALU.max))
                        step(dve, dve.tensor_scalar(coarse[:, :, :], coarse_16[:, :, :], 0.25, None,
                                                    ALU.mult))
                        shape = [P, B, rounds, NCTX // P]
                        step(dve, dve.tensor_tensor(mask_bias[:, :, :, :],
                                                    cols[:, :, :].unsqueeze(2).to_broadcast(shape),
                                                    coarse[:, :, :].unsqueeze(2).to_broadcast(shape),
                                                    ALU.subtract))
                        dve.sem_inc(m.ready.sem, 1)

                    @block.sync
                    def _(sp):
                        sp.wait_ge(m.ready.sem, m.ready.at(1))
                        rounds = PAIRS // 2 // B
                        for b in range(B):
                            sp.dma_start(mask_scr[b * rounds:(b + 1) * rounds, :]
                                         .rearrange("(o r) k -> o r k", o=1),
                                         mask_row[0:1, b:b + 1, :].to_broadcast([1, rounds, NCTX]))\
                              .then_inc(m.stored.sem, 16)
                        sp.wait_ge(m.stored.sem, m.stored.at(16 * B))
                m.ready.close(1)
                m.stored.close(16 * B)
                q_t = pair_of("q_t", [P, KC, T], scope)
                k_t = pair_of("k_t", [P, KC, B * NCTX], scope)
                project_transposed(m, wq, x_views, q_t, KC, T, qb)
                project_transposed(m, wk, c_t, k_t, KC, B * NCTX, kb)
                project_narrow_values(m, wv, c_t, values, B * NCTX // P, ones_row[:, :], vb[:, :])
                store_heads(m, q_t, (0, 1, 0), q0_scr, NQ)
                store_heads(m, k_t, (0, 0, 1), k0_scr, NCTX)
            if stop > 1:
                narrow_attention(m, ident[:, :], fold[:, :], q0_scr, k0_scr, values, result, NCTX, mask_scr,
                                 mask_bias[:, :, :, :].rearrange("p b r t -> p (b r t)"))

            def self_output(prefix, out_dst=z):
                with ExitStack() as scope:
                    w, = split_weights([prefix + "_w"], KC, scope)
                    b = sb(prefix + "_b", [1, D], F32, scope)
                    g = sb(prefix + "_g", [P, D], F32, scope)
                    be = sb(prefix + "_be", [P, D], F32, scope)
                    load_all([(b[:, :], row(prefix + "_b")), (g[:, :], everywhere(prefix + "_g")),
                              (be[:, :], everywhere(prefix + "_be"))])
                    project_tokens(m, w, x_views, [P] * KC, D, add_residual, ones_row[:, :], b[:, :])
                    layer_norm(m, tmp, z, z, g[:, :], be[:, :])

            def head_source(t, c):
                first = (t // QT) * 16 + 8 * c
                return result[:, t % QT, first:first + 8, :].rearrange("p h d -> p (h d)")

            if stop > 1:
                transpose_split(m, ident[:, :], head_source, [P] * KC, *x_views)
                self_output("L0_xattn_co")
            if stop > 2:
                to_x_t()
                values1 = sb("values1", [P, PAIRS, NQ // P, V_COLS], F32, s_ctx)
                with ExitStack() as scope:
                    wq, wk, wv = split_weights(["L0_xattn_sq_w", "L0_xattn_sk_w", "L0_xattn_sv_w"], KC, scope)
                    qb = sb("sqb", [P, KC], F32, scope)
                    kb = sb("skb", [P, KC], F32, scope)
                    vb = sb("svb", [1, D], F32, scope)
                    load_all([(qb[:, :], column("L0_xattn_sq_b")), (kb[:, :], column("L0_xattn_sk_b")),
                              (vb[:, :], row("L0_xattn_sv_b"))])
                    q_t = pair_of("sq_t", [P, KC, T], scope)
                    k_t = pair_of("sk_t", [P, KC, T], scope)
                    project_transposed(m, wq, x_views, q_t, KC, T, qb)
                    project_transposed(m, wk, x_views, k_t, KC, T, kb)
                    project_narrow_values(m, wv, x_views, values1, TT, ones_row[:, :], vb[:, :])
                    store_heads(m, q_t, (0, 1, 0), q0_scr, NQ)
                    store_heads(m, k_t, (0, 0, 1), k1_scr, NQ)
                narrow_attention(m, ident[:, :], fold[:, :], q0_scr, k1_scr, values1, result, NQ)
                transpose_split(m, ident[:, :], head_source, [P] * KC, *x_views)
                self_output("L0_xattn_so")
        if stop > 3:
            to_x_t()
            with ExitStack() as scope:
                fi, = split_weights(["L0_xattn_fi_w"], KC, scope)
                fo, = split_weights(["L0_xattn_fo_w"], 8, scope)
                fib = sb("fib", [P, 8], F32, scope)
                b = sb("fob", [1, D], F32, scope)
                g = sb("fog", [P, D], F32, scope)
                be = sb("fobe", [P, D], F32, scope)
                load_all([(fib[:, :], column("L0_xattn_fi_b")), (b[:, :], row("L0_xattn_fo_b")),
                          (g[:, :], everywhere("L0_xattn_fo_g")), (be[:, :], everywhere("L0_xattn_fo_be"))])
                hid = pair_of("gelu", [P, 8, T], scope)
                feed_forward_gelu(m, fi, x_views, hid, fib, 8)
                project_tokens(m, fo, hid, [P] * 8, D, add_residual, ones_row[:, :], b[:, :])
                layer_norm(m, tmp, z, z, g[:, :], be[:, :])
            with m.block() as block:
                @block.vector
                def _(dve):
                    for t in range(TT):
                        dve.scalar_tensor_tensor(res[:, t, :], z[:, t, :], tanh_g[:, 0:1], res[:, t, :],
                                                 ALU.mult, ALU.add)
        if stop > 4:
            with ExitStack() as scope:
                quant_ctx = ExitStack()
                wg_t = pair_of("wg_t", [P, KC, FFN_H], scope)
                wu_t = pair_of("wu_t", [P, KC, FFN_H], scope)
                wd_t = pair_of("wd_t", [P, 6, D], scope)
                hid = sb("ffn_hid", [P, TT, FFN_H], F32, scope)
                tmp["amax"] = sb("amax", [P, 6 * D // 16], F32, scope)
                tmp["inv"] = sb("inv", [P, 6 * D // 16], F32, scope)
                tmp["quant"] = sb("quant", [P, 4, 6 * D], F32, scope)
                with ExitStack() as ws:
                    wg = sb("wg", [P, 6, D], F32, ws)
                    wu = sb("wu", [P, 6, D], F32, ws)
                    wd = sb("wd", [P, KC, FFN_H], F32, ws)
                    items = []
                    for dst, name in ((wg, "L0_ffn_w_gate"), (wu, "L0_ffn_w_up")):
                        items.append((dst[:, 0:5, :], a[name][0:640, :].rearrange("(c p) n -> p c n", p=P)))
                        items.append((dst[0:64, 5, :], a[name][640:704, :]))
                    items.append((wd[:, :, :], weight("L0_ffn_w_down")))
                    load_all(items)
                    views = []
                    for wt in (wg, wu):
                        views.append((wt[:, 0:5, :].rearrange("p c (n b) -> p (c n) b", b=16), 80))
                        views.append((wt[0:64, 5, :].rearrange("p (n b) -> p n b", b=16), 16))
                    for c in range(KC):
                        views.append((wd[:, c, :].rearrange("p (n b) -> p n b", b=16), FFN_BLOCKS))
                    with m.block() as block:
                        @block.vector
                        def _(dve):
                            for v, n in views:
                                quantise(m, tmp, v, v, n)(dve)
                    for wt, dst in ((wg, wg_t), (wu, wu_t)):
                        turn_weight(m, ident, wt, FFN_ROWS, KC, dst)
                    turn_weight(m, ident, wd, [P] * KC, 6, wd_t, FFN_ROWS)
                layer_norm(m, tmp, res, z)
                with m.block() as block:
                    @block.vector
                    def _(dve):
                        for t in range(0, TT, 4):
                            v = z[:, t:t + 4, :].rearrange("p t (n b) -> p (t n) b", b=16)
                            quantise(m, tmp, v, v, 64)(dve)
                to_x_t()
                gate_up(m, x_views, wg_t, wu_t, hid)
                with m.block() as block:
                    @block.vector
                    def _(dve):
                        for t in range(0, TT, 2):
                            v = hid[:, t:t + 2, :].rearrange("p t (n b) -> p (t n) b", b=16)
                            quantise(m, tmp, v, v, 2 * FFN_BLOCKS)(dve)
                h_t = pair_of("hid_t", [P, 6, T], scope)
                transpose_split(m, ident[:, :],
                                lambda t, c: hid[:, t, c * P:c * P + FFN_ROWS[c]], FFN_ROWS, *h_t)
                project_tokens(m, wd_t, h_t, FFN_ROWS, D, gated(2))
        if stop > 5:
            layer_norm(m, tmp, res, z)
            to_x_t()
            with ExitStack() as s_ctx:
                values = sb("values2", [P, B, 8, NCTX // P, 129], F16, s_ctx)
                result = sb("heads_out2", [P, QT, B * 8, 64], F32, s_ctx)
                with ExitStack() as scope:
                    c_t = split_weights(["ctx_t"], KC, scope)[0]
                    wq, = split_weights(["L1_xattn_Wq"], KC, scope)
                    with ExitStack() as s:
                        q_t = pair_of("q2_t", [P, 4, T], s)
                        project_transposed(m, wq, x_views, q_t, 4, T)
                        store_heads(m, q_t, (0, 1), q2_scr, NQ)
                    wk, = split_weights(["L1_xattn_Wk"], KC, scope)
                    with ExitStack() as s:
                        k_t = pair_of("k2_t", [P, 4, B * NCTX], s)
                        project_transposed(m, wk, c_t, k_t, 4, B * NCTX)
                        store_heads(m, k_t, (0, 1), k2_scr, NCTX)
                    wv, = split_weights(["L1_xattn_Wv"], KC, scope)
                    project_values(m, wv, c_t, values, B * NCTX // P, 8, 64)
                wide_attention(m, ident[:, :], q2_scr, k2_scr, values, result, NCTX, 8, 64)
                with ExitStack() as scope:
                    a_t = pair_of("a2_t", [P, 4, T], scope)
                    transpose_split(m, ident[:, :],
                                    lambda t, c: result[:, t % QT, (t // QT) * 8 + 2 * c:
                                                        (t // QT) * 8 + 2 * c + 2, :]
                                    .rearrange("p h d -> p (h d)"), [P] * 4, *a_t)
                    wo, = split_weights(["L1_xattn_Wo"], 4, scope)
                    b = sb("bo", [1, D], F32, scope)
                    load_all([(b[:, :], row("L1_xattn_bo"))])
                    project_tokens(m, wo, a_t, [P] * 4, D, gated(1), ones_row[:, :], b[:, :])
        if stop > 6:
            layer_norm(m, tmp, res, z)
            to_x_t()
            with ExitStack() as scope:
                gate = sb("gate", [P, TT, EXPERTS], F32, scope)
                weights = sb("expert_weights", [P, SLOTS, TT], F32, scope)
                with ExitStack() as s:
                    wr, = split_weights(["L1_ffn_Wg_t"], KC, s)
                    rb = sb("rb", [1, EXPERTS], F32, s)
                    load_all([(rb[:, :], row("L1_ffn_routing_bias"))])

                    def keep_gate(dve, t, view):
                        dve.tensor_copy(gate[:, t, :], view)

                    project_tokens(m, wr, x_views, [P] * KC, EXPERTS, keep_gate, ones_row[:, :], rb[:, :])
                route(m, tmp, gate, weights)
                acc = sb("acc", [P, TT, D], F32, scope)
                mixture(m, x_views, a["moe_w12"], a["moe_w3"], weights, acc)
                with m.block() as block:
                    @block.vector
                    def _(dve):
                        for t in range(TT):
                            dve.scalar_tensor_tensor(res[:, t, :], acc[:, t, :], tanh_g[:, 3:4],
                                                     res[:, t, :], ALU.mult, ALU.add)
        with m.block() as block:
            @block.sync
            def _(sp):
                shown = res if stop in (4, 5, 6, 7, 99) else z
                sp.dma_start(out.rearrange("b (t p) d -> p (b t) d", p=P), shown[:, :, :])\
                  .then_inc(m.stored.sem, 16)
                sp.wait_ge(m.stored.sem, m.stored.at(16))


def turn_weight(m, ident, src, row_chunks, col_chunks, dst, col_sizes=None):
    sizes = col_sizes or [P] * col_chunks
    groups = [(c, r) for c in range(col_chunks) for r in range(0, len(row_chunks), 4)]
    with m.block() as block:
        def extent(c, r):
            rows = row_chunks[r:r + 4]
            return sizes[c], r * P, sum(rows)

        @block.tensor
        def _(pe):
            for g, (c, r) in enumerate(groups):
                if g >= 8:
                    pe.wait_ge(m.low_done.sem, m.low_done.at(g - 7))
                for j, rows in enumerate(row_chunks[r:r + 4]):
                    ins = pe.transpose(m.psum[0:sizes[c], g % 8, j * P:j * P + rows],
                                       src[0:rows, r + j, c * P:c * P + sizes[c]], ident[0:rows, 0:rows])
                ins.then_inc(m.products.sem, 1)

        @block.scalar
        def _(act):
            for g, (c, r) in enumerate(groups):
                n, at, size = extent(c, r)
                act.wait_ge(m.products.sem, m.products.at(g + 1))
                act.activation(dst[0][0:n, c, at:at + size], m.psum[0:n, g % 8, 0:size],
                               ACT.Copy).then_inc(m.high_done.sem, 1)

        @block.vector
        def _(dve):
            for g, (c, r) in enumerate(groups):
                n, at, size = extent(c, r)
                dve.wait_ge(m.high_done.sem, m.high_done.at(g + 1))
                dve.tensor_tensor(dst[1][0:n, c, at:at + size], m.psum[0:n, g % 8, 0:size],
                                  dst[0][0:n, c, at:at + size], ALU.subtract).then_inc(m.low_done.sem, 1)

    m.products.close(len(groups))
    m.high_done.close(len(groups))
    m.low_done.close(len(groups))


STOP = 99


def kernel(**inputs):
    import numpy as np
    import concourse.bacc as bacc
    from concourse import mybir as _mybir
    from concourse.bass_utils import run_bass_kernel_spmd

    arrays = {k: np.asarray(v) for k, v in inputs.items()}
    moved = ["ctx_1024", "L1_ffn_Wg", "L1_ffn_W1", "L1_ffn_W2", "L1_ffn_W3", "L1_ffn_Ws1", "L1_ffn_Ws2",
             "L1_ffn_Ws3"]
    laid = {k: v for k, v in arrays.items() if k not in moved}
    laid["ctx_t"] = arrays["ctx_1024"].reshape(-1, 256).T
    laid["mask_columns"] = arrays["mask_Bx1x1xS2_ff0"].reshape(-1, 128).T
    for name in ("cq_b", "ck_b", "sq_b", "sk_b", "fi_b"):
        laid[f"L0_xattn_{name}_columns"] = laid.pop("L0_xattn_" + name).reshape(-1, 128).T
    laid["L1_ffn_Wg_t"] = arrays["L1_ffn_Wg"].T
    w1 = np.concatenate([arrays["L1_ffn_Ws1"][None], arrays["L1_ffn_W1"]])
    w2 = np.concatenate([arrays["L1_ffn_Ws2"][None], arrays["L1_ffn_W2"]])
    w3 = np.concatenate([arrays["L1_ffn_Ws3"][None], arrays["L1_ffn_W3"]])
    w12 = np.stack([w1, w2], 1)
    w12 = w12.transpose(0, 3, 1, 2).reshape(9, 2, 128, 2, 682)
    laid["moe_w12"] = w12.transpose(0, 2, 1, 3, 4).reshape(9, 128, 4 * 682)
    laid["moe_w3"] = w3.transpose(0, 2, 1)
    laid["identity"] = np.eye(128, dtype=np.float32)
    nc = bacc.Bacc("TRN2", target_bir_lowering=False, num_devices=1)
    feeds, aps = {}, {}
    for name, v in laid.items():
        v = np.ascontiguousarray(v)
        feeds["in_" + name] = v
        aps[name] = nc.dram_tensor("in_" + name, v.shape, _mybir.dt.from_np(v.dtype),
                                   kind="ExternalInput").ap()
    out = nc.dram_tensor("out_x", (2, 512, 256), _mybir.dt.float32, kind="ExternalOutput").ap()
    flamingo_gated_kernel(nc, aps, out, STOP)
    got = run_bass_kernel_spmd(nc, [feeds], core_ids=[0])
    return got.results[0]["out_x"]
```
